# Optimizing a Trainium2 kernel written in Bass

```python
import numpy as np
import jax
import jax.numpy as jnp

def _softmax(x, axis=-1):
    return jax.nn.softmax(x, axis=axis)

def _gelu(x):
    return jax.nn.gelu(x, approximate=True)

def _silu(x):
    return jax.nn.silu(x)

def _sigmoid(x):
    return jax.nn.sigmoid(x)

def _layernorm(x, axis=-1, eps=1e-05):
    m = jnp.mean(x, axis=axis, keepdims=True)
    v = jnp.var(x, axis=axis, keepdims=True)
    return (x - m) / jnp.sqrt(v + eps)

def _scatter_add(tgt, idx, src, axis=0):
    return tgt.at[idx].add(src)

def _segment_sum(src, seg, n):
    return jax.ops.segment_sum(src, seg, n)
kernel_name = 'mk_decoder_preln_d1_seqx_r4_4fdc66'

def setup_inputs(seed: int=0):
    np.random.seed(seed)
    _w = jnp.asarray

    def _rec_inputs():
        import jax
        import jax.numpy as jnp
        _rk = jax.random.key(seed)
        x = 7.22e-05 + 1 * jax.random.normal(jax.random.fold_in(_rk, 1), (16, 256, 256), jnp.float32)
        _lenS = 256 - jax.random.randint(jax.random.fold_in(_rk, 7), (16,), 0, max(1, 256 // 4) + 1, jnp.int32)
        _lenS2 = 77 - jax.random.randint(jax.random.fold_in(_rk, 8), (16,), 0, max(1, 77 // 4) + 1, jnp.int32)
        _ctx_1024P = jax.random.normal(jax.random.fold_in(_rk, 11), (16, 16, 256), jnp.float32)
        _ctx_1024c = jax.random.dirichlet(jax.random.fold_in(_rk, 511), 0.3 * jnp.ones((16,), jnp.float32), (16, 77))
        _ctx_1024t = jnp.einsum('bsk,bkd->bsd', _ctx_1024c, _ctx_1024P)
        _ctx_1024t = _ctx_1024t * jax.lax.rsqrt(jnp.mean(jnp.square(_ctx_1024t)) + 1e-12) * 0.953939
        ctx_1024 = 4.13588e-05 + 0.999923 * (_ctx_1024t + 0.3 * jax.random.normal(jax.random.fold_in(_rk, 611), (16, 77, 256), jnp.float32))
        return (x, ctx_1024)
    x, ctx_1024 = _rec_inputs()

    def _L0_attn_setup():
        import jax, jax.numpy as jnp
        import numpy as np
        EPS = 1e-06
        key = jax.random.key(seed)
        kx, kw = jax.random.split(key)
        B, L, D = (4, 2048, 256)
        x = jax.random.normal(kx, (B, L, D), dtype=jnp.float32)
        W = jax.random.normal(kw, (D, 3 * D), dtype=jnp.float32) * 0.02
        return {'x': x, 'W': W}
    _L0_attn_all = _L0_attn_setup()
    _L0_attn_in = {k: v for k, v in _L0_attn_all.items() if k in ('W',)}
    del _L0_attn_all

    def _L0_xattn_setup():
        import jax, jax.numpy as jnp
        import numpy as np
        B, LQ, LK = (4, 512, 512)
        DQ, DK, DO = (256, 256, 256)
        key = jax.random.key(seed)
        ks = jax.random.split(key, 9)
        s = 0.02
        return {'query_input': jax.random.normal(ks[0], (B, LQ, DQ), jnp.float32), 'key_input': jax.random.normal(ks[1], (B, LK, DK), jnp.float32), 'value_input': jax.random.normal(ks[2], (B, LK, DK), jnp.float32), 'Wq': jax.random.normal(ks[3], (DQ, DO), jnp.float32) * s, 'bq': jax.random.normal(ks[4], (DO,), jnp.float32) * s, 'Wk': jax.random.normal(ks[5], (DK, DO), jnp.float32) * s, 'bk': jax.random.normal(ks[6], (DO,), jnp.float32) * s, 'Wv': jax.random.normal(ks[7], (DK, DO), jnp.float32) * s, 'bv': jax.random.normal(ks[8], (DO,), jnp.float32) * s}
    _L0_xattn_all = _L0_xattn_setup()
    _L0_xattn_in = {k: v for k, v in _L0_xattn_all.items() if k in ('Wq', 'bq', 'Wk', 'bk', 'Wv', 'bv')}
    del _L0_xattn_all

    def _L0_ffn_setup():
        import jax, jax.numpy as jnp
        import numpy as np
        import math
        N_EMBD = 256
        HIDDEN = 4 * N_EMBD
        N_EXPERTS = 8
        TOP_K = 2
        B, T = (4, 512)

        def new_gelu(x):
            c = math.sqrt(2.0 / math.pi)
            return 0.5 * x * (1.0 + jnp.tanh(c * (x + 0.044715 * x * x * x)))

        def _moe_forward(x, Wfc_s, bfc_s, Wproj_s, bproj_s, Wr, Wfc, bfc, Wproj, bproj):
            Bb, Tt, C = x.shape
            xf = x.reshape(Bb * Tt, C)
            N = Bb * Tt
            shared = new_gelu(xf @ Wfc_s + bfc_s) @ Wproj_s + bproj_s
            logits = xf @ Wr
            probs = jax.nn.softmax(logits, axis=-1)
            topk_p, topk_i = jax.lax.top_k(probs, TOP_K)
            topk_p = topk_p / jnp.sum(topk_p, axis=-1, keepdims=True)
            gate = jnp.zeros((N, N_EXPERTS), dtype=xf.dtype)
            gate = gate.at[jnp.arange(N)[:, None], topk_i].add(topk_p)
            routed = jnp.zeros_like(xf)
            for e in range(N_EXPERTS):
                h = new_gelu(xf @ Wfc[e] + bfc[e]) @ Wproj[e] + bproj[e]
                routed = routed + h * gate[:, e:e + 1]
            return (shared + routed).reshape(Bb, Tt, C)
        key = jax.random.key(seed)
        ks = jax.random.split(key, 10)
        s = 0.02
        return {'x': jax.random.normal(ks[0], (B, T, N_EMBD), dtype=jnp.float32), 'Wfc_s': jax.random.normal(ks[1], (N_EMBD, HIDDEN), dtype=jnp.float32) * s, 'bfc_s': jnp.zeros((HIDDEN,), dtype=jnp.float32), 'Wproj_s': jax.random.normal(ks[2], (HIDDEN, N_EMBD), dtype=jnp.float32) * s, 'bproj_s': jnp.zeros((N_EMBD,), dtype=jnp.float32), 'Wr': jax.random.normal(ks[3], (N_EMBD, N_EXPERTS), dtype=jnp.float32) * s, 'Wfc': jax.random.normal(ks[4], (N_EXPERTS, N_EMBD, HIDDEN), dtype=jnp.float32) * s, 'bfc': jnp.zeros((N_EXPERTS, HIDDEN), dtype=jnp.float32), 'Wproj': jax.random.normal(ks[5], (N_EXPERTS, HIDDEN, N_EMBD), dtype=jnp.float32) * s, 'bproj': jnp.zeros((N_EXPERTS, N_EMBD), dtype=jnp.float32)}
    _L0_ffn_all = _L0_ffn_setup()
    _L0_ffn_in = {k: v for k, v in _L0_ffn_all.items() if k in ('Wfc_s', 'bfc_s', 'Wproj_s', 'bproj_s', 'Wr', 'Wfc', 'bfc', 'Wproj', 'bproj')}
    del _L0_ffn_all
    return {'x': x, 'ctx_1024': ctx_1024, 'L0_attn_W': _L0_attn_in['W'], 'L0_xattn_Wq': _L0_xattn_in['Wq'], 'L0_xattn_bq': _L0_xattn_in['bq'], 'L0_xattn_Wk': _L0_xattn_in['Wk'], 'L0_xattn_bk': _L0_xattn_in['bk'], 'L0_xattn_Wv': _L0_xattn_in['Wv'], 'L0_xattn_bv': _L0_xattn_in['bv'], 'L0_ffn_Wfc_s': _L0_ffn_in['Wfc_s'], 'L0_ffn_bfc_s': _L0_ffn_in['bfc_s'], 'L0_ffn_Wproj_s': _L0_ffn_in['Wproj_s'], 'L0_ffn_bproj_s': _L0_ffn_in['bproj_s'], 'L0_ffn_Wr': _L0_ffn_in['Wr'], 'L0_ffn_Wfc': _L0_ffn_in['Wfc'], 'L0_ffn_bfc': _L0_ffn_in['bfc'], 'L0_ffn_Wproj': _L0_ffn_in['Wproj'], 'L0_ffn_bproj': _L0_ffn_in['bproj']}

def reference(x, ctx_1024, L0_attn_W, L0_xattn_Wq, L0_xattn_bq, L0_xattn_Wk, L0_xattn_bk, L0_xattn_Wv, L0_xattn_bv, L0_ffn_Wfc_s, L0_ffn_bfc_s, L0_ffn_Wproj_s, L0_ffn_bproj_s, L0_ffn_Wr, L0_ffn_Wfc, L0_ffn_bfc, L0_ffn_Wproj, L0_ffn_bproj):
    import jax
    import jax.numpy as jnp

    def _L0_attn_ref(x, W):
        import jax, jax.numpy as jnp
        import numpy as np
        EPS = 1e-06
        D = x.shape[-1]
        qkv = x @ W
        q, k, v = jnp.split(qkv, 3, axis=-1)
        q = jax.nn.elu(q) + 1.0
        k = jax.nn.elu(k) + 1.0
        KV = jnp.einsum('bld,blh->bhd', k, v)
        k_sum = k.sum(axis=1)
        Z = 1.0 / (jnp.einsum('bld,bd->bl', q, k_sum) + EPS)
        V = jnp.einsum('bld,bhd,bl->blh', q, KV, Z)
        return V

    def _L0_xattn_ref(query_input, key_input, value_input, Wq, bq, Wk, bk, Wv, bv):
        import jax, jax.numpy as jnp
        import numpy as np
        B, LQ, LK = (4, 512, 512)
        DQ, DK, DO = (256, 256, 256)
        scale = jnp.asarray(DO, query_input.dtype) ** 0.5
        q = query_input @ Wq + bq
        k = key_input @ Wk + bk
        v = value_input @ Wv + bv
        attn = jnp.einsum('bqd,bkd->bqk', q, k) / scale
        attn = jax.nn.softmax(attn, axis=-1)
        return jnp.einsum('bqk,bkd->bqd', attn, v)

    def _L0_ffn_ref(x, Wfc_s, bfc_s, Wproj_s, bproj_s, Wr, Wfc, bfc, Wproj, bproj):
        import jax, jax.numpy as jnp
        import numpy as np
        import math
        N_EMBD = 256
        HIDDEN = 4 * N_EMBD
        N_EXPERTS = 8
        TOP_K = 2
        B, T = (4, 512)

        def new_gelu(x):
            c = math.sqrt(2.0 / math.pi)
            return 0.5 * x * (1.0 + jnp.tanh(c * (x + 0.044715 * x * x * x)))

        def _moe_forward(x, Wfc_s, bfc_s, Wproj_s, bproj_s, Wr, Wfc, bfc, Wproj, bproj):
            Bb, Tt, C = x.shape
            xf = x.reshape(Bb * Tt, C)
            N = Bb * Tt
            shared = new_gelu(xf @ Wfc_s + bfc_s) @ Wproj_s + bproj_s
            logits = xf @ Wr
            probs = jax.nn.softmax(logits, axis=-1)
            topk_p, topk_i = jax.lax.top_k(probs, TOP_K)
            topk_p = topk_p / jnp.sum(topk_p, axis=-1, keepdims=True)
            gate = jnp.zeros((N, N_EXPERTS), dtype=xf.dtype)
            gate = gate.at[jnp.arange(N)[:, None], topk_i].add(topk_p)
            routed = jnp.zeros_like(xf)
            for e in range(N_EXPERTS):
                h = new_gelu(xf @ Wfc[e] + bfc[e]) @ Wproj[e] + bproj[e]
                routed = routed + h * gate[:, e:e + 1]
            return (shared + routed).reshape(Bb, Tt, C)
        return _moe_forward(x, Wfc_s, bfc_s, Wproj_s, bproj_s, Wr, Wfc, bfc, Wproj, bproj)
    x = x + _L0_attn_ref(_layernorm(x, axis=-1), L0_attn_W)
    x = x + _L0_xattn_ref(_layernorm(x, axis=-1), ctx_1024, ctx_1024, L0_xattn_Wq, L0_xattn_bq, L0_xattn_Wk, L0_xattn_bk, L0_xattn_Wv, L0_xattn_bv)
    x = x + _L0_ffn_ref(_layernorm(x, axis=-1), L0_ffn_Wfc_s, L0_ffn_bfc_s, L0_ffn_Wproj_s, L0_ffn_bproj_s, L0_ffn_Wr, L0_ffn_Wfc, L0_ffn_bfc, L0_ffn_Wproj, L0_ffn_bproj)
    return x

_drawn_inputs = setup_inputs


def setup_inputs(seed=0):
    import zlib

    import numpy as np

    out = dict(_drawn_inputs(seed))
    spreads = {'L0_ffn_bfc_s': (0.0, 0.1),
     'L0_ffn_bproj_s': (0.0, 0.1),
     'L0_ffn_bfc': (0.0, 0.327),
     'L0_ffn_bproj': (0.0, 0.1)}
    factors = {'L0_xattn_Wq': 6.103, 'L0_xattn_bq': 8.0, 'L0_xattn_Wk': 6.236, 'L0_xattn_bk': 8.0}
    for name, (base, spread) in spreads.items():
        noise = np.random.default_rng([zlib.crc32(name.encode()), seed]).standard_normal(out[name].shape)
        drawn = base * np.exp(spread * noise) if base else spread * noise
        out[name] = jnp.asarray(drawn.astype(out[name].dtype))
    for name, factor in factors.items():
        out[name] = (out[name] * factor).astype(out[name].dtype)
    return out
```

```python
from contextlib import ExitStack

import concourse.bass as bass
from concourse import mybir

F32 = mybir.dt.float32
F16 = mybir.dt.float16
I32 = mybir.dt.int32
U32 = mybir.dt.uint32
ALU = mybir.AluOpType
ACT = mybir.ActivationFunctionType
AX = mybir.AxisListType
ds = bass.ds

P = 128
LN_EPS = 1e-5
ATTN_EPS = 1e-6
W_SCALE = 256.0
A_SCALE = 16.0
UNSCALE = 1.0 / (W_SCALE * A_SCALE)
LAG = 4


def decoder_layer(nc, x, ctx_in, attn_w, wq_in, bq_in, wk_in, bk_in, wv_in, bv_in,
                  fc_s, bfc_s, proj_s, bproj_s, wr_in, fc, bfc, proj, bproj, out):
    B, S, D = x.shape
    CK = ctx_in.shape[1]
    E, _, H = fc.shape
    T = B * S
    TB = S // P
    TILES = T // P
    DK = D // P
    FC = H // P
    BLK = S
    NSH = T // BLK
    NRT = 2 * T // BLK + E - 1
    NBLK = NSH + NRT
    ROW = D + E + 1
    HALVES = 2 * (E + 1)
    SCALE = float(D) ** -0.5
    assert S == 256 and D == 256 and H == 1024 and CK <= P

    rows_dram = nc.dram_tensor("rows_by_expert", [NRT * BLK, ROW], F32).ap()
    x2_dram = nc.dram_tensor("x2_residual", [T, D], F32).ap()

    def tiles_of(ap, b):
        return ap.rearrange("(b t p) n -> b p t n", t=TB, p=P)[ds(b, 1)].rearrange("b p t n -> p (b t) n")

    out_rows = out.rearrange("b s d -> (b s) d")
    x_rows = x.rearrange("b s d -> (b s) d")

    with ExitStack() as stack:
        def sb(name, shape, dt):
            return stack.enter_context(nc.sbuf_tensor(name, shape, dt))

        def pb(name, shape, dt=F32):
            return stack.enter_context(nc.psum_tensor(name, shape, dt))

        def sem(name):
            return stack.enter_context(nc.semaphore(name))

        w1 = sb("w1_parts", [P, HALVES * 2048], F16)
        w2 = sb("w2_parts", [P, HALVES * 2048], F16)
        rows = sb("rows", [P, TILES, ROW], F32)
        rows16 = rows[:, :, :].bitcast(F16)
        rows_i = rows[:, :, :].bitcast(I32)
        stage1 = sb("stage_w1", [P, 1024], F32)
        stage2 = sb("stage_w2", [P, 4, 256], F32)
        ident = sb("ident", [P, P], F32)
        ident16 = sb("ident16", [P, P], F16)
        earlier = sb("earlier", [P, P], F16)
        ones16 = sb("ones16", [P, P], F16)
        NB1 = (E + 1) * FC
        bias_cols = sb("bias_columns", [P, NB1 + 2 * DK], F32)
        bq = bias_cols[:, NB1:NB1 + DK]
        bk = bias_cols[:, NB1 + DK:NB1 + 2 * DK]
        stats = sb("stats", [P, 3, TB, 6], F32)
        mv = sb("mean_var", [P, 3, TB, 2], F32)
        var_eps = sb("var_eps", [P, 3 * TB], F32)
        minus_half = sb("minus_half", [P, 3 * TB], F32)
        carrier = sb("wait_carrier", [P, 1], F32)
        rstd = sb("rstd", [P, 3 * TB], F32)
        nmax = sb("nmax", [P, TB], F32)
        nbias = sb("nbias", [P, TB], F32)
        psum_p = sb("p_sum", [P, TB], F32)
        rinv = sb("rinv", [P, TB], F32)
        zden = sb("z_den", [P, TB], F32)
        zinv = sb("z_inv", [P, TB], F32)
        lg = sb("logits", [P, TB, E], F32)
        max8 = sb("max8", [P, TB, 8], F32)
        max8_at = sb("max8_at", [P, TB, 8], U32)
        top = sb("top_values", [P, TILES, 2], F32)
        top_f = sb("top_experts", [P, TILES, 2], F32)
        dest = sb("dest_rows", [P, 2, TILES], I32)
        blk_expert = sb("block_expert", [P, NRT], I32)

        FW = ROW * TB + 512 + 1024 + 512 + 1024 + 512 + 256
        fbuf = sb("expert_buffers", [P, FW], F32)
        at = [0]

        def cut(n):
            at[0] += n
            return fbuf[:, at[0] - n:at[0]]

        xrow = cut(ROW * TB).rearrange("p (t w) -> p t w", t=TB)
        x2blk = cut(512).rearrange("p (t n) -> p t n", t=TB)
        xT = [cut(512).bitcast(F16).rearrange("p (k l n) -> p k l n", k=DK, l=2) for _ in range(2)]
        g32 = [cut(256) for _ in range(2)]
        gs = [cut(256).bitcast(F16).rearrange("p (l n) -> p l n", l=2) for _ in range(4)]
        ybuf = cut(512).rearrange("p (t n) -> p t n", t=TB)
        b2blk = cut(256)
        gate = [sb(f"gate{i}", [P, TB], F32) for i in range(2)]
        token = [sb(f"token{i}", [P, TB], I32) for i in range(2)]

        last = (HALVES - 6) * 2048
        tail1 = w1[:, last:last + 4 * 2048].bitcast(F32)
        tail2 = w2[:, last:last + 4 * 2048].bitcast(F32)
        regions = [[tail1, 0, 4096], [tail2, 0, 4096], [fbuf, 0, FW]]

        def lend(n, pattern=None, **dims):
            for r in regions:
                if r[2] - r[1] >= n:
                    r[1] += n
                    ap = r[0][:, r[1] - n:r[1]]
                    return ap.rearrange(pattern, **dims) if pattern else ap
            raise ValueError("no room")

        wqkv = lend(DK * 3 * D, "p (k n) -> p k n", k=DK)
        wq = lend(DK * D, "p (k n) -> p k n", k=DK)
        wk = lend(DK * D, "p (k n) -> p k n", k=DK)
        wv = lend(DK * D, "p (k n) -> p k n", k=DK)
        xn = [lend(TB * D, "p (t n) -> p t n", t=TB) for _ in range(3)]
        xnT = [lend(DK * S, "p (k n) -> p k n", k=DK) for _ in range(3)]
        expk = lend(TB * D, "p (t n) -> p t n", t=TB)
        expq = lend(DK * S, "p (k n) -> p k n", k=DK)
        kfeat = lend(TB * D, "p (t n) -> p t n", t=TB)
        qfeatT = lend(DK * S, "p (k n) -> p k n", k=DK)
        q2T = lend(DK * S, "p (k n) -> p k n", k=DK)
        vones = lend(TB * (D + 1), "p (t n) -> p t n", t=TB)
        state = lend(DK * (D + 1), "p (k n) -> p k n", k=DK)
        ctx_sb = lend(D)
        ctxT = lend(DK * CK, "p (k n) -> p k n", k=DK)
        k2T = lend(DK * CK, "p (k n) -> p k n", k=DK)
        v2 = lend(D)
        bv = lend(D)
        prob = lend(TB * CK, "p (t n) -> p t n", t=TB)
        probT = lend(S)
        wr = lend(DK * E, "p (k n) -> p k n", k=DK)
        pad_row = lend(ROW)
        bias_rows = lend(P)

        route = [[tail2, 0, 4096]]

        def scratch(n):
            route[0][1] += n
            return tail2[:, route[0][1] - n:route[0][1]]

        TE = TILES * E

        def te(ap):
            return ap.rearrange("p (t e) -> p t e", e=E)

        hot = [te(scratch(TE)) for _ in range(2)]
        gated = te(scratch(TE))
        picked = scratch(TE).bitcast(F16)[:, 0:TE]
        iota_te = te(scratch(TE))
        iota_i = scratch(TE).bitcast(I32)
        dlog = scratch(TILES)
        edlog = scratch(TILES)
        gden = scratch(TILES)
        g1 = scratch(TILES)
        g2 = scratch(TILES)
        totals = scratch(TE).rearrange("p (e t) -> p e t", e=E)
        keep = scratch(TE).rearrange("p (e t) -> p e t", e=E)
        upto = scratch(TE).rearrange("p (e t) -> p e t", e=E)
        base = scratch(TE).rearrange("p (e t) -> p e t", e=E)
        place = te(scratch(TE))
        chosen = te(scratch(TE))
        dest_f = scratch(2 * TILES).rearrange("p (j t) -> p j t", j=2)
        nblk_i = scratch(E).bitcast(I32)
        nblk_i2 = scratch(E).bitcast(I32)
        nblk = scratch(E)
        ones_e = scratch(E)
        blk_end = scratch(E)
        first_row = scratch(E)
        past = scratch(NRT * E).rearrange("p (n e) -> p n e", e=E)
        iota_blk = scratch(NRT)
        iota_blk_i = scratch(NRT).bitcast(I32)
        blk_f = scratch(NRT)

        bank0 = pb("bank0", [P, 512])
        bank_kv = pb("bank_kv", [P, 2, 512])
        bank3 = pb("bank3", [P, 512])
        bank_st = pb("bank_st", [P, 2, 512])
        bank6 = pb("bank6", [P, 512])
        bank7 = pb("bank7", [P, 512])

        tr = bank0[:, :].rearrange("p (k n) -> p k n", k=DK)
        qps = bank3[:, :].rearrange("p (k n) -> p k n", k=DK)
        q2ps = bank6[:, :].rearrange("p (k n) -> p k n", k=DK)
        ctxT_ps = bank7[:, 0:DK * CK].rearrange("p (k n) -> p k n", k=DK)
        k2T_ps = bank7[:, 256:256 + DK * CK].rearrange("p (k n) -> p k n", k=DK)
        v2_ps = bank7[:, 0:D]
        sc_ps = bank7[:, 0:TB * CK].rearrange("p (t n) -> p t n", t=TB)
        pT_ps = bank7[:, 0:S]
        pv_ps = bank_kv[:, 0, :].rearrange("p (t n) -> p t n", t=TB)
        lg_ps = bank_kv[:, 1, 0:TB * E].rearrange("p (t n) -> p t n", t=TB)
        count_ps = bank6[:, :].rearrange("p (j n) -> p j n", j=2)
        hid = [bank0, bank3]
        ypair = [bank_kv, bank_st]
        rowT_ps = bank7[:, :].bitcast(F16)

        s = {}
        for name in ("const_loaded x_loaded ctx_loaded w1_loaded w2_loaded x2_stored pads_stored "
                     "ident16_set ones_set ident_set pow_set biasT_done bias_ready "
                     "stats_part var_ready rstd_ready xn1_ready xn2_ready xn3_ready "
                     "t1_done t2_done t3_done t1_copied t2_copied t3_copied "
                     "kv_done q_done expk_ready v_copied expq_ready kmin kfeat_ready qmin qfeat_ready "
                     "state_done state_copied attn_done z_step x1_ready "
                     "ctxT_done ctxT_copied k2v2_done k2_ready v2_ready q2_done q2_ready "
                     "scores_done smax_step smax_ready p_ready rinv_ready pT_done pT_copied pv_done x2_ready "
                     "logits_done logits_copied max_step top_step top_ready hi_step xf_ready w_hi w_lo "
                     "route_step route_iota exp_gate counts_done picked_ready routed rows_sent "
                     "up_done gelu_done g_hi g_ready down_done y_read y_ready rowT_done xT_ready "
                     "meta_taken carried xrow_loaded x2blk_loaded b2_loaded y_stored y_added").split():
            s[name] = sem(name)

        block = stack.enter_context(nc.Block())

        def live(b):
            return not isinstance(b, int) or 0 <= b < B

        def got(eng, name, b):
            eng.wait_ge(s[name], b + 1)

        def got_if(eng, name, b):
            if isinstance(b, int):
                b = min(b, B - 1)
                if b < 0:
                    return
            eng.wait_ge(s[name], b + 1)

        def apart(eng):
            eng.wait_ge(s["const_loaded"], 10 * 16)

        def steps(eng, step, ahead=1):
            for i in range(-1, LAG + 1):
                step(i)
            with eng.Fori(LAG + 1, B - ahead) as i:
                step(i)
            for i in range(B - ahead, B + LAG):
                step(i)

        def half_of(i):
            if isinstance(i, int) and not LAG <= i < B:
                return 2 * E + i if i in (0, 1) else None
            return i - LAG

        def part_count(i):
            if isinstance(i, int) and not LAG <= i < B:
                return min(max(i, 0), 2)
            return i - (LAG - 2)

        def stream(eng, body):
            body(0, 0, False, None)
            body(1, 1, False, "shared")
            with eng.Fori(1, NSH // 2 - 1) as j:
                for c in range(2):
                    body(2 * j + c, c, False, "shared")
            body(NSH - 2, 0, False, "shared")
            body(NSH - 1, 1, False, "shared")
            body(NSH, 0, True, "shared")
            body(NSH + 1, 1, True, "routed")
            with eng.Fori(1, NRT // 2) as j:
                for c in range(2):
                    body(2 * j + (NSH + c), c, True, "routed")
            body(NBLK - 1, 0, True, "routed")

        def is_last(G):
            return isinstance(G, int) and G == NBLK - 1

        def next_kind(G, routed):
            if is_last(G):
                return None
            return "routed" if routed or (isinstance(G, int) and G == NSH - 1) else "shared"

        @block.sync
        def _(sp):
            def load(dst, src):
                sp.dma_start(dst, src).then_inc(s["const_loaded"], 16)

            sp.dma_start(rows[:, 0:TB, 0:D], tiles_of(x_rows, 0)).then_inc(s["x_loaded"], 16)
            load(wqkv, attn_w.rearrange("(k p) n -> p k n", p=P))
            load(wq, wq_in.rearrange("(k p) n -> p k n", p=P))
            load(wk, wk_in.rearrange("(k p) n -> p k n", p=P))
            load(wv, wv_in.rearrange("(k p) n -> p k n", p=P))
            load(wr, wr_in.rearrange("(k p) n -> p k n", p=P))
            load(bias_rows[0:E * FC, :], bfc.rearrange("e (c p) -> (e c) p", p=P))
            load(bias_rows[E * FC:NB1, :], bfc_s.rearrange("(c p) -> c p", p=P))
            load(bias_rows[NB1:NB1 + DK, :], bq_in.rearrange("(k p) -> k p", p=P))
            load(bias_rows[NB1 + DK:NB1 + 2 * DK, :], bk_in.rearrange("(k p) -> k p", p=P))
            load(bv, bv_in.rearrange("(a n) -> a n", a=1).broadcast_to([P, D]))
            w1_half = fc.rearrange("e (k p) f -> (e k) p f", p=P)
            w2_half = proj.rearrange("e (h c p) n -> (e h) p c n", p=P, c=4)
            w1_shared = fc_s.rearrange("(k p) f -> k p f", p=P)
            w2_shared = proj_s.rearrange("(h c p) n -> h p c n", p=P, c=4)

            def load_half(half, before):
                shared = isinstance(half, int) and half >= 2 * E
                a = w1_shared[half - 2 * E] if shared else w1_half[ds(half, 1)].rearrange("a p f -> p (a f)")
                c = w2_shared[half - 2 * E] if shared else w2_half[ds(half, 1)].rearrange("a p c n -> p (a c) n")
                sp.wait_ge(s["w_lo"], before)
                sp.dma_start(stage1[:, :], a).then_inc(s["w1_loaded"], 16)
                sp.dma_start(stage2[:, :, :], c).then_inc(s["w2_loaded"], 16)

            def step(i):
                if (half := half_of(i)) is not None:
                    load_half(half, part_count(i))
                b = i + 2
                if (isinstance(b, int) and 1 <= b < B) or not isinstance(b, int):
                    sp.wait_ge(s["x_loaded"], b * 16)
                    sp.dma_start(rows[:, ds(b * TB, TB), 0:D], tiles_of(x_rows, b)).then_inc(s["x_loaded"], 16)
                if live(i - 1):
                    b = i - 1
                    sp.wait_ge(s["ctxT_done"], b)
                    sp.dma_start(ctx_sb[0:CK, :], ctx_in[ds(b, 1)].rearrange("b s d -> s (b d)"))\
                        .then_inc(s["ctx_loaded"], 16)
                if live(i - 3):
                    b = i - 3
                    got(sp, "x2_ready", b)
                    sp.wait_ge(s["x2_stored"], b * 16)
                    sp.dma_start(tiles_of(x2_dram, b), rows[:, ds(b * TB, TB), 0:D])\
                        .then_inc(s["x2_stored"], 16)

            steps(sp, step, ahead=2)

            sp.wait_ge(s["logits_done"], B)
            sp.wait_ge(s["pads_stored"], 16)

            def load_b2(G, e):
                sp.wait_ge(s["y_read"], G)
                src = bproj_s.rearrange("(a n) -> a n", a=1) if isinstance(e, int) else bproj[ds(e, 1)]
                sp.dma_start(b2blk, src.broadcast_to([P, D])).then_inc(s["b2_loaded"], 16)

            def finish_shared(G):
                got(sp, "y_ready", G)
                sp.dma_start(tiles_of(out_rows, G), ybuf).then_inc(s["y_stored"], 16)

            def shared_block(G):
                if isinstance(G, int) and G == 0:
                    sp.wait_ge(s["x2_stored"], B * 16)
                else:
                    sp.wait_ge(s["y_ready"], G)
                sp.dma_start(x2blk, tiles_of(x2_dram, G)).then_inc(s["x2blk_loaded"], 16)
                load_b2(G, E)
                if not (isinstance(G, int) and G == 0):
                    finish_shared(G - 1)

            def last_halves(k):
                for q in range(k, k + 2):
                    load_half(2 * E - 4 + q, B - LAG + 2 + q)

            last_halves(0)
            shared_block(0)
            with sp.Fori(0, (NSH - 2) // 2) as j:
                for c in range(2):
                    shared_block(2 * j + (1 + c))
            shared_block(NSH - 1)
            last_halves(2)

            sp.wait_ge(s["routed"], 1)
            sp.wait_ge(s["rows_sent"], 2 * TILES * 16)

            def load_rows(n):
                sp.wait_ge(s["meta_taken"], n)
                sp.dma_start(xrow, tiles_of(rows_dram, n)).then_inc(s["xrow_loaded"], 16)

            def expert_of(n):
                return sp.value_load(blk_expert[0:1, ds(n, 1)], min_val=0, max_val=E - 1)

            load_rows(0)
            load_b2(NSH, expert_of(0))
            finish_shared(NSH - 1)
            load_rows(1)
            with sp.Fori(1, NRT - 1) as n:
                load_b2(n + NSH, expert_of(n))
                load_rows(n + 1)
            load_b2(NRT - 1 + NSH, expert_of(NRT - 1))

        @block.gpsimd
        def _(pool):
            pool.memset(minus_half[:, :], -0.5)
            pool.memset(pad_row, 0.0).then_inc(s["pow_set"], 1)
            pool.memset(ident[:, :], 0.0).then_inc(s["pow_set"], 1)
            pool.memset(earlier[:, :], 1.0).then_inc(s["pow_set"], 1)
            pool.wait_ge(s["pow_set"], 2)
            pool.affine_select(out=ident[:, :], in_=ident[:, :], compare_op=ALU.not_equal, fill=1.0,
                               base=0, pattern=[[-1, P]], channel_multiplier=1).then_inc(s["ident_set"], 1)
            pool.memset(pad_row.bitcast(I32)[:, ROW - 1:ROW], T).then_inc(s["pow_set"], 1)
            pool.wait_ge(s["pow_set"], 4)
            pool.dma_start(rows_dram.rearrange("(n p) w -> p n w", p=P),
                           pad_row.rearrange("p (n w) -> p n w", n=1).broadcast_to([P, NRT * TB, ROW]))\
                .then_inc(s["pads_stored"], 16)
            pool.affine_select(out=earlier[:, :], in_=earlier[:, :], compare_op=ALU.is_gt, fill=0.0,
                               base=0, pattern=[[1, P]], channel_multiplier=-1).then_inc(s["ident_set"], 1)
            pool.wait_ge(s["ident_set"], 1)
            pool.tensor_copy(ident16[:, :], ident[:, :]).then_inc(s["ident16_set"], 1)

            def step(k):
                pool.wait_ge(s["var_ready"], k + 1)
                pool.tensor_tensor(rstd[:, :], var_eps[:, :], minus_half[:, :], ALU.pow).then_inc(s["rstd_ready"], 1)

            with pool.Fori(0, B + LAG) as k:
                step(k)

            pool.wait_ge(s["logits_done"], B)
            pool.wait_ge(s["xf_ready"], B)
            pool.iota(iota_i, [[0, TILES], [1, E]], base=0, channel_multiplier=0).then_inc(s["route_iota"], 1)
            pool.iota(iota_blk_i, [[1, NRT]], base=0, channel_multiplier=0).then_inc(s["route_iota"], 1)
            pool.memset(keep, 1.0).then_inc(s["route_iota"], 1)
            pool.memset(ones_e, 1.0)
            pool.wait_ge(s["route_iota"], 3)
            pool.memset(keep[:, :, 0:1], 0.0).then_inc(s["route_iota"], 1)
            pool.iota(rows_i[:, :, ROW - 1], [[P, TILES]], base=0, channel_multiplier=1)\
                .then_inc(s["route_iota"], 1)

            pool.wait_ge(s["route_iota"], 5)
            pool.wait_ge(s["routed"], 1)
            pool.wait_ge(s["pads_stored"], 16)
            for t in range(TILES):
                for j in range(2):
                    pool.indirect_dma_start(
                        out=rows_dram, out_offset=bass.IndirectOffsetOnAxis(ap=dest[:, j, t:t + 1].bitcast(U32), axis=0),
                        in_=rows[:, t, :], in_offset=None).then_inc(s["rows_sent"], 16)

            last_token = pool.to_reg(T - 1)

            def add_block(n, parity):
                pool.wait_ge(s["y_ready"], n + (NSH + 1))
                pool.wait_ge(s["carried"], n)
                if isinstance(n, int) and n == 0:
                    pool.wait_ge(s["y_stored"], NSH * 16)
                else:
                    pool.wait_ge(s["y_added"], n * (16 * TB))
                pool.tensor_tensor(carrier[:, :], minus_half[:, 0:1], minus_half[:, 0:1], ALU.add)\
                    .then_inc(s["carried"], 1)
                for t in range(TB):
                    pool.indirect_dma_start(
                        out=out_rows, out_offset=bass.IndirectOffsetOnAxis(ap=token[parity][:, t:t + 1].bitcast(U32), axis=0),
                        in_=ybuf[:, t, :], in_offset=None, bounds_check=last_token, oob_is_err=False,
                        compute_op=ALU.add).then_inc(s["y_added"], 16)

            add_block(0, 0)
            with pool.Fori(0, (NRT - 1) // 2) as j:
                for c in range(2):
                    add_block(2 * j + (1 + c), (1 + c) % 2)
            pool.wait_ge(s["y_added"], NRT * TB * 16)

        @block.scalar
        def _(act):
            def copy(dst, src, name):
                act.activation(dst, src, ACT.Copy).then_inc(s[name], 1)

            def convert_hi(half, before):
                act.wait_ge(s["w1_loaded"], (before + 1) * 16)
                act.wait_ge(s["w2_loaded"], (before + 1) * 16)
                act.activation(w1[:, ds(half * 2048, 1024)], stage1[:, :], ACT.Copy, scale=W_SCALE)
                act.activation(w2[:, ds(half * 2048, 1024)], stage2[:, :, :].rearrange("p c n -> p (c n)"),
                               ACT.Copy, scale=W_SCALE).then_inc(s["w_hi"], 1)

            def step(i):
                if live(i - 3):
                    b = i - 3
                    got(act, "smax_ready", b)
                    got_if(act, "pT_done", b - 1)
                    for t in range(TB):
                        op = act.activation(prob[:, t, :], sc_ps[:, t, :], ACT.Exp, bias=nbias[:, t:t + 1],
                                            scale=SCALE, accum_out=psum_p[:, t:t + 1])
                    op.then_inc(s["p_ready"], 1)
                if live(i):
                    got(act, "t1_done", i)
                    copy(xnT[0], tr, "t1_copied")
                if live(i - 1):
                    got(act, "state_done", i - 1)
                    copy(state, bank_st[:, :, 0:D + 1], "state_copied")
                if live(i):
                    got(act, "kv_done", i)
                    got_if(act, "kfeat_ready", i - 1)
                    act.activation(expk, bank_kv[:, :, 0:D], ACT.Exp).then_inc(s["expk_ready"], 1)
                    copy(vones[:, :, 0:D], bank_kv[:, :, D:2 * D], "v_copied")
                    got(act, "q_done", i)
                    got_if(act, "qfeat_ready", i - 1)
                    act.activation(expq, qps, ACT.Exp).then_inc(s["expq_ready"], 1)
                if live(i - 3):
                    got(act, "pT_done", i - 3)
                    got_if(act, "pv_done", i - 4)
                    copy(probT[0:CK, :], pT_ps[0:CK, :], "pT_copied")
                if live(i - 2):
                    got(act, "t2_done", i - 2)
                    copy(xnT[1], tr, "t2_copied")
                    got(act, "ctxT_done", i - 2)
                    copy(ctxT, ctxT_ps, "ctxT_copied")
                if live(i - 4):
                    got(act, "t3_done", i - 4)
                    copy(xnT[2], tr, "t3_copied")
                if live(i - 2):
                    got(act, "k2v2_done", i - 2)
                    for m in range(DK):
                        op = act.activation(k2T[:, m, :], k2T_ps[:, m, :], ACT.Identity, bias=bk[:, m:m + 1])
                    op.then_inc(s["k2_ready"], 1)
                    got(act, "q2_done", i - 2)
                    for m in range(DK):
                        op = act.activation(q2T[:, m, :], q2ps[:, m, :], ACT.Identity, bias=bq[:, m:m + 1])
                    op.then_inc(s["q2_ready"], 1)
                if (half := half_of(i)) is not None:
                    convert_hi(half, part_count(i))

            act.wait_ge(s["biasT_done"], 1)
            copy(bias_cols[:, :], q2ps.rearrange("p k n -> p (k n)")[:, 0:NB1 + 2 * DK], "bias_ready")
            act.wait_ge(s["bias_ready"], 1)
            steps(act, step)

            act.wait_ge(s["route_step"], 1)
            act.activation(edlog, dlog, ACT.Exp).then_inc(s["exp_gate"], 1)

            def body(G, parity, routed, before):
                e = E
                if routed:
                    e = act.value_load(blk_expert[0:1, ds(G - NSH, 1)], min_val=0, max_val=E - 1)
                for f in range(FC):
                    got(act, "up_done", FC * G + f)
                    if not (isinstance(G, int) and FC * G + f < 2):
                        act.wait_ge(s["g_ready"], FC * G + (f - 1))
                    bias = bias_cols[:, ds(e * FC + f, 1)]
                    act.activation(g32[f % 2], hid[f % 2][:, 0:BLK], ACT.Gelu_apprx_tanh, bias=bias,
                                   scale=UNSCALE).then_inc(s["gelu_done"], 1)
                    if f == 5 and not is_last(G):
                        got(act, "rowT_done", G + 1)
                        copy(xT[1 - parity].rearrange("p k l n -> p (k l n)"), rowT_ps, "xT_ready")
                    if isinstance(G, int) and G in (0, NSH - 1) and f in (2, 6):
                        q = 2 * (G > 0) + (f == 6)
                        act.wait_ge(s["routed"], 1)
                        convert_hi(2 * E - 4 + q, B - LAG + 2 + q)

            act.wait_ge(s["logits_done"], B)
            got(act, "rowT_done", 0)
            copy(xT[0].rearrange("p k l n -> p (k l n)"), rowT_ps, "xT_ready")
            stream(act, body)

        @block.vector
        def _(dve):
            route_count = [0]

            def chain(op, name, count, own=False):
                op.then_inc(s[name], 1)
                if own:
                    apart(dve)
                dve.wait_ge(s[name], count)

            def convert_lo(half, before):
                dve.wait_ge(s["w_hi"], before + 1)
                for w, stage in ((w1, stage1[:, :]), (w2, stage2[:, :, :].rearrange("p c n -> p (c n)"))):
                    op = dve.scalar_tensor_tensor(w[:, ds(half * 2048 + 1024, 1024)], stage, W_SCALE,
                                                  w[:, ds(half * 2048, 1024)], ALU.mult, ALU.subtract)
                op.then_inc(s["w_lo"], 1)

            def step(i):
                if live(i - 3):
                    b = i - 3
                    got(dve, "scores_done", b)
                    got_if(dve, "p_ready", b - 1)
                    chain(dve.reduce_max(nmax[:, :], sc_ps, AX.X, negate=True), "smax_step", b + 1)
                    dve.tensor_scalar(nbias[:, :], nmax[:, :], SCALE, None, ALU.mult).then_inc(s["smax_ready"], 1)
                if live(i):
                    got(dve, "expk_ready", i)
                    chain(dve.tensor_scalar(expk, expk, 1.0, None, ALU.min), "kmin", i + 1)
                    got(dve, "v_copied", i)
                    got_if(dve, "state_done", i - 1)
                    dve.scalar_tensor_tensor(kfeat, bank_kv[:, :, 0:D], 1.0, expk, ALU.add, ALU.max)\
                        .then_inc(s["kfeat_ready"], 1)
                if live(i - 3):
                    got(dve, "p_ready", i - 3)
                    dve.reciprocal(rinv[:, :], psum_p[:, :]).then_inc(s["rinv_ready"], 1)
                if live(i - 1):
                    b = i - 1
                    got(dve, "attn_done", b)
                    chain(dve.tensor_scalar(zden[:, :], bank_st[:, :, D], ATTN_EPS, None, ALU.add),
                          "z_step", 2 * b + 1)
                    chain(dve.reciprocal(zinv[:, :], zden[:, :]), "z_step", 2 * b + 2)
                    for t in range(TB):
                        r = rows[:, ds(b * TB + t, 1), 0:D].rearrange("p a n -> p (a n)")
                        op = dve.scalar_tensor_tensor(r, bank_st[:, t, 0:D], zinv[:, t:t + 1], r, ALU.mult, ALU.add)
                    op.then_inc(s["x1_ready"], 1)
                if live(i):
                    got(dve, "expq_ready", i)
                    chain(dve.tensor_scalar(expq, expq, 1.0, None, ALU.min), "qmin", i + 1)
                    dve.scalar_tensor_tensor(qfeatT, qps, 1.0, expq, ALU.add, ALU.max).then_inc(s["qfeat_ready"], 1)
                if live(i - 3):
                    b = i - 3
                    got(dve, "rinv_ready", b)
                    got(dve, "pv_done", b)
                    for t in range(TB):
                        r = rows[:, ds(b * TB + t, 1), 0:D].rearrange("p a n -> p (a n)")
                        op = dve.scalar_tensor_tensor(r, pv_ps[:, t, :], rinv[:, t:t + 1], r, ALU.mult, ALU.add)
                    op.then_inc(s["x2_ready"], 1)
                if live(i - 2):
                    b = i - 2
                    got(dve, "k2_ready", b)
                    dve.tensor_tensor(v2[0:CK, :], v2_ps[0:CK, :], bv[0:CK, :], ALU.add).then_inc(s["v2_ready"], 1)

                norms = [(0, i + 1), (1, i - 1), (2, i - 3)]
                norms = [(n, b) for n, b in norms if live(b)]
                if norms:
                    k = i + 1
                    for n, b in norms:
                        apart(dve)
                        if n == 0:
                            dve.wait_ge(s["x_loaded"], (b + 1) * 16)
                        else:
                            got(dve, "x1_ready" if n == 1 else "x2_ready", b)
                        for t in range(TB):
                            r = rows[:, ds(b * TB + t, 1), 0:D].rearrange("p a n -> p (a n)")
                            op = dve.bn_stats(stats[:, n, t, :], r)
                    chain(op, "stats_part", 2 * k + 1, own=True)
                    for n, b in norms:
                        for t in range(TB):
                            op = dve.bn_aggr(mv[:, n, t, :], stats[:, n, t, :])
                    chain(op, "stats_part", 2 * k + 2)
                    dve.tensor_scalar(var_eps[:, :].rearrange("p (n t) -> p n t", n=3), mv[:, :, :, 1], LN_EPS, None,
                                      ALU.add).then_inc(s["var_ready"], 1)
                if live(i - 4):
                    b = i - 4
                    got(dve, "logits_done", b)
                    chain(dve.tensor_copy(lg[:, :, :], lg_ps), "logits_copied", b + 1, own=True)
                    for t in range(TB):
                        op = dve.max(max8[:, t, :], lg[:, t, :])
                    chain(op, "max_step", b + 1, own=True)
                    for t in range(TB):
                        op = dve.max_index(max8_at[:, t, :], max8[:, t, :], lg[:, t, :])
                    chain(op, "top_step", b + 1)
                    dve.tensor_copy(top[:, ds(b * TB, TB), :], max8[:, :, 0:2])
                    dve.tensor_copy(top_f[:, ds(b * TB, TB), :], max8_at[:, :, 0:2]).then_inc(s["top_ready"], 1)
                    dve.wait_ge(s["x2_stored"], (b + 1) * 16)
                    hi = rows16[:, ds(b * TB, TB), 0:D]
                    lo = rows16[:, ds(b * TB, TB), D:2 * D]
                    chain(dve.tensor_scalar(hi, xn[2], A_SCALE, None, ALU.mult), "hi_step", b + 1)
                    dve.scalar_tensor_tensor(lo, xn[2], A_SCALE, hi, ALU.mult, ALU.subtract).then_inc(s["xf_ready"], 1)
                if norms:
                    dve.wait_ge(s["rstd_ready"], k + 1)
                    for n, b in norms:
                        got_if(dve, f"t{n + 1}_done", b - 1)
                        if n == 2:
                            got_if(dve, "xf_ready", b - 1)
                        for t in range(TB):
                            r = rows[:, ds(b * TB + t, 1), 0:D].rearrange("p a n -> p (a n)")
                            op = dve.tensor_scalar(xn[n][:, t, :], r, mv[:, n, t, 0:1],
                                                   rstd[:, n * TB + t:n * TB + t + 1], ALU.subtract, ALU.mult)
                        op.then_inc(s[f"xn{n + 1}_ready"], 1)
                if (half := half_of(i)) is not None:
                    convert_lo(half, part_count(i))

            dve.memset(mv[:, :, :, :], 1.0)
            dve.memset(vones[:, :, D:D + 1], 1.0)
            dve.memset(ones16[:, :], 1.0).then_inc(s["ones_set"], 1)
            dve.wait_ge(s["ones_set"], 1)
            dve.wait_ge(s["const_loaded"], 10 * 16)
            steps(dve, step)

            def then(op):
                route_count[0] += 1
                chain(op, "route_step", route_count[0])

            def over_e(ap):
                return ap.rearrange("p (t a) -> p t a", a=1).broadcast_to([P, TILES, E])

            dve.wait_ge(s["top_ready"], B)
            dve.wait_ge(s["w_lo"], 2 + B - LAG)
            then(dve.tensor_tensor(dlog, top[:, :, 1], top[:, :, 0], ALU.subtract))
            dve.wait_ge(s["route_iota"], 4)
            dve.tensor_copy(iota_te.rearrange("p t e -> p (t e)"), iota_i)
            then(dve.tensor_copy(iota_blk, iota_blk_i))
            for j in range(2):
                op = dve.tensor_tensor(hot[j], iota_te, top_f[:, :, j:j + 1].broadcast_to([P, TILES, E]), ALU.is_equal)
            then(op)
            dve.tensor_tensor(picked.rearrange("p (t e) -> p t e", e=E), hot[0], hot[1], ALU.add)\
                .then_inc(s["picked_ready"], 1)
            dve.wait_ge(s["exp_gate"], 1)
            then(dve.tensor_scalar(gden, edlog, 1.0, None, ALU.add))
            then(dve.reciprocal(g1, gden))
            then(dve.tensor_tensor(g2, g1, edlog, ALU.mult))
            dve.tensor_tensor(gated, hot[0], over_e(g1), ALU.mult)
            then(dve.tensor_tensor(chosen, hot[1], over_e(g2), ALU.mult))
            dve.wait_ge(s["xf_ready"], B)
            then(dve.tensor_tensor(rows[:, :, D:D + E], gated, chosen, ALU.add))
            dve.wait_ge(s["counts_done"], 1)
            then(dve.tensor_copy(totals, count_ps[:, 1, :].rearrange("p (t e) -> p e t", e=E)))
            then(dve.tensor_tensor_scan(upto.rearrange("p e t -> p (e t)"), keep.rearrange("p e t -> p (e t)"),
                                        totals.rearrange("p e t -> p (e t)"), 0.0, ALU.mult, ALU.add))
            then(dve.tensor_scalar(nblk_i, upto[:, :, TILES - 1], float(BLK - 1), None, ALU.add))
            then(dve.tensor_scalar(nblk_i2, nblk_i, BLK.bit_length() - 1, None, ALU.logical_shift_right))
            then(dve.tensor_copy(nblk, nblk_i2))
            then(dve.tensor_tensor_scan(blk_end, ones_e, nblk, 0.0, ALU.mult, ALU.add))
            then(dve.tensor_tensor(first_row, blk_end, nblk, ALU.subtract))
            dve.tensor_tensor(base, upto, totals, ALU.subtract)
            then(dve.tensor_tensor(past, iota_blk.rearrange("p (n a) -> p n a", a=1).broadcast_to([P, NRT, E]),
                                   blk_end.rearrange("p (a e) -> p a e", a=1).broadcast_to([P, NRT, E]), ALU.is_ge))
            then(dve.tensor_reduce(blk_f, past, AX.X, ALU.add))
            dve.tensor_scalar(blk_expert[:, :], blk_f, float(E - 1), None, ALU.min)
            then(dve.scalar_tensor_tensor(
                base, first_row.rearrange("p (e a) -> p e a", a=1).broadcast_to([P, E, TILES]), float(BLK),
                base, ALU.mult, ALU.add))
            then(dve.tensor_tensor(place, te(count_ps[:, 0, :]), base.rearrange("p e t -> p t e"), ALU.add))
            for j in range(2):
                then(dve.tensor_tensor(chosen, place, hot[j], ALU.mult))
                then(dve.tensor_reduce(dest_f[:, j, :], chosen, AX.X, ALU.add))
            dve.tensor_copy(dest[:, :, :], dest_f).then_inc(s["routed"], 1)

            def evacuate(G, parity, shared):
                dve.wait_ge(s["down_done"], FC * (G + 1))
                dve.wait_ge(s["b2_loaded"], 16 * (G + 1))
                if not (isinstance(G, int) and G == 0):
                    if shared or (isinstance(G, int) and G == NSH):
                        dve.wait_ge(s["y_stored"], 16 * G)
                    else:
                        dve.wait_ge(s["y_added"], (16 * TB) * (G - NSH))
                for t in range(TB):
                    op = dve.scalar_tensor_tensor(ybuf[:, t, :], ypair[parity][:, t, 0:D], UNSCALE, b2blk,
                                                  ALU.mult, ALU.add)
                op.then_inc(s["y_read"], 1)
                dve.wait_ge(s["y_read"], G + 1)
                if shared:
                    dve.wait_ge(s["x2blk_loaded"], 16 * (G + 1))
                    dve.tensor_tensor(ybuf, ybuf, x2blk, ALU.add).then_inc(s["y_ready"], 1)
                else:
                    for t in range(TB):
                        op = dve.tensor_scalar(ybuf[:, t, :], ybuf[:, t, :], gate[parity][:, t:t + 1], None, ALU.mult)
                    op.then_inc(s["y_ready"], 1)

            def body(G, parity, routed, before):
                for f in range(FC):
                    c = FC * G + f
                    got(dve, "gelu_done", c)
                    if not (isinstance(c, int) and c < 4):
                        dve.wait_ge(s["down_done"], c - 3)
                    g = gs[f % 4]
                    chain(dve.tensor_scalar(g[:, 0, :], g32[f % 2], A_SCALE, None, ALU.mult), "g_hi", c + 1)
                    dve.scalar_tensor_tensor(g[:, 1, :], g32[f % 2], A_SCALE, g[:, 0, :], ALU.mult, ALU.subtract)\
                        .then_inc(s["g_ready"], 1)
                    if f == 2 and not (isinstance(G, int) and G == 0):
                        evacuate(G - 1, 1 - parity, shared=before == "shared")
                    if f == 6 and next_kind(G, routed) == "routed":
                        n = G + (1 - NSH)
                        expert = dve.value_load(blk_expert[0:1, ds(n, 1)], min_val=0, max_val=E - 1)
                        got(dve, "rowT_done", G + 1)
                        if not (isinstance(n, int) and n < 2):
                            dve.wait_ge(s["y_added"], (n - 1) * (16 * TB))
                        dve.tensor_copy(gate[1 - parity][:, :],
                                        xrow[:, :, ds(expert + D, 1)].rearrange("p t a -> p (t a)"))
                        dve.tensor_copy(token[1 - parity][:, :], xrow[:, :, ROW - 1].bitcast(I32))\
                            .then_inc(s["meta_taken"], 1)
                    if isinstance(G, int) and G in (0, NSH - 1) and f in (2, 6):
                        q = 2 * (G > 0) + (f == 6)
                        convert_lo(2 * E - 4 + q, B - LAG + 2 + q)

            dve.wait_ge(s["routed"], 1)
            stream(dve, body)
            evacuate(NBLK - 1, 0, shared=False)

        @block.tensor
        def _(pe):
            def tile(t):
                return slice(t * P, (t + 1) * P)

            def transpose_norm(n):
                for t in range(TB):
                    for k in range(DK):
                        op = pe.transpose(tr[:, k, tile(t)], xn[n][:, t, tile(k)], ident[:, :])
                return op

            def step(i):
                if live(i - 3):
                    b = i - 3
                    got(pe, "q2_ready", b)
                    got(pe, "v2_ready", b)
                    for t in range(TB):
                        for m in range(DK):
                            op = pe.matmul(sc_ps[:, t, :], q2T[:, m, tile(t)], k2T[:, m, :], start=m == 0, stop=m == DK - 1)
                    op.then_inc(s["scores_done"], 1)
                if live(i):
                    got(pe, "xn1_ready", i)
                    got_if(pe, "t3_copied", i - 5)
                    transpose_norm(0).then_inc(s["t1_done"], 1)
                if live(i - 1):
                    b = i - 1
                    got(pe, "kfeat_ready", b)
                    got_if(pe, "x1_ready", b - 1)
                    for m in range(DK):
                        for t in range(TB):
                            op = pe.matmul(bank_st[:, m, 0:D + 1], kfeat[:, t, tile(m)], vones[:, t, :],
                                           start=t == 0, stop=t == TB - 1)
                    op.then_inc(s["state_done"], 1)
                if live(i):
                    got(pe, "t1_copied", i)
                    got_if(pe, "x2_ready", i - 4)
                    got_if(pe, "logits_copied", i - 5)
                    for t in range(TB):
                        for k in range(DK):
                            op = pe.matmul(bank_kv[:, t, :], xnT[0][:, k, tile(t)], wqkv[:, k, D:3 * D],
                                           start=k == 0, stop=k == DK - 1)
                    op.then_inc(s["kv_done"], 1)
                    got_if(pe, "qfeat_ready", i - 1)
                    for m in range(DK):
                        for k in range(DK):
                            op = pe.matmul(qps[:, m, :], wqkv[:, k, tile(m)], xnT[0][:, k, :],
                                           start=k == 0, stop=k == DK - 1)
                    op.then_inc(s["q_done"], 1)
                if live(i - 3):
                    got(pe, "p_ready", i - 3)
                    for t in range(TB):
                        op = pe.transpose(pT_ps[0:CK, tile(t)], prob[:, t, :], ident[:, :])
                    op.then_inc(s["pT_done"], 1)
                if live(i - 2):
                    got(pe, "xn2_ready", i - 2)
                    got_if(pe, "t1_copied", i)
                    transpose_norm(1).then_inc(s["t2_done"], 1)
                if live(i - 1):
                    b = i - 1
                    got(pe, "state_copied", b)
                    got(pe, "qfeat_ready", b)
                    for t in range(TB):
                        for m in range(DK):
                            op = pe.matmul(bank_st[:, t, 0:D + 1], qfeatT[:, m, tile(t)], state[:, m, :],
                                           start=m == 0, stop=m == DK - 1)
                    op.then_inc(s["attn_done"], 1)
                if live(i - 2):
                    b = i - 2
                    pe.wait_ge(s["ctx_loaded"], (b + 1) * 16)
                    got_if(pe, "pT_copied", b - 1)
                    for k in range(DK):
                        op = pe.transpose(ctxT_ps[:, k, :], ctx_sb[0:CK, tile(k)], ident[0:CK, 0:CK])
                    op.then_inc(s["ctxT_done"], 1)
                if live(i - 3):
                    b = i - 3
                    got(pe, "pT_copied", b)
                    got_if(pe, "kfeat_ready", i)
                    for t in range(TB):
                        op = pe.matmul(pv_ps[:, t, :], probT[0:CK, tile(t)], v2[0:CK, :], start=True, stop=True)
                    op.then_inc(s["pv_done"], 1)
                if live(i - 4):
                    got(pe, "xn3_ready", i - 4)
                    got_if(pe, "t2_copied", i - 2)
                    transpose_norm(2).then_inc(s["t3_done"], 1)
                if live(i - 2):
                    b = i - 2
                    got(pe, "ctxT_copied", b)
                    for m in range(DK):
                        for k in range(DK):
                            pe.matmul(k2T_ps[:, m, :], wk[:, k, tile(m)], ctxT[:, k, :], start=k == 0, stop=k == DK - 1)
                    for k in range(DK):
                        op = pe.matmul(v2_ps[0:CK, :], ctxT[:, k, :], wv[:, k, :], start=k == 0, stop=k == DK - 1)
                    op.then_inc(s["k2v2_done"], 1)
                    got(pe, "t2_copied", b)
                    got_if(pe, "q2_ready", b - 1)
                    for m in range(DK):
                        for k in range(DK):
                            op = pe.matmul(q2ps[:, m, :], wq[:, k, tile(m)], xnT[1][:, k, :], start=k == 0, stop=k == DK - 1)
                    op.then_inc(s["q2_done"], 1)
                if live(i - 4):
                    got(pe, "t3_copied", i - 4)
                    got_if(pe, "kfeat_ready", i)
                    for t in range(TB):
                        for k in range(DK):
                            op = pe.matmul(lg_ps[:, t, :], xnT[2][:, k, tile(t)], wr[:, k, :], start=k == 0, stop=k == DK - 1)
                    op.then_inc(s["logits_done"], 1)

            pe.wait_ge(s["const_loaded"], 10 * 16)
            pe.wait_ge(s["ident_set"], 2)
            pe.wait_ge(s["ident16_set"], 1)
            pe.wait_ge(s["ones_set"], 1)
            n = NB1 + 2 * DK
            pe.transpose(bank6[:, 0:n], bias_rows[0:n, :], ident[0:n, 0:n]).then_inc(s["biasT_done"], 1)
            pe.wait_ge(s["bias_ready"], 1)
            steps(pe, step)

            def transpose_rows(source):
                for k in range(DK):
                    for part in range(2):
                        for t in range(TB):
                            at = ((k * 2 + part) * TB + t) * P
                            op = pe.transpose(rowT_ps[:, at:at + P], source(t, part, k), ident16[:, :])
                op.then_inc(s["rowT_done"], 1)

            def shared_source(G):
                def source(t, part, k):
                    at = part * D + k * P
                    return rows16[:, ds(G * TB + t, 1), at:at + P].rearrange("p a n -> p (a n)")
                return source

            xrow16 = xrow.bitcast(F16)

            def routed_source(t, part, k):
                at = part * D + k * P
                return xrow16[:, t, at:at + P]

            def up(G, parity, e, f):
                c = FC * G + f
                if not (isinstance(c, int) and c < 2):
                    pe.wait_ge(s["gelu_done"], c - 1)
                x = xT[parity]
                for k in range(DK):
                    w_hi, w_lo = (w1[:, ds(e * 4096 + (k * 2048 + part * 1024 + f * P), P)] for part in range(2))
                    pe.matmul(hid[f % 2][:, 0:BLK], w_hi, x[:, k, 0, :], start=k == 0, stop=False)
                    pe.matmul(hid[f % 2][:, 0:BLK], w_hi, x[:, k, 1, :], start=False, stop=False)
                    op = pe.matmul(hid[f % 2][:, 0:BLK], w_lo, x[:, k, 0, :], start=False, stop=k == DK - 1)
                op.then_inc(s["up_done"], 1)

            def down(G, parity, e, f):
                c = FC * G + f
                got(pe, "g_ready", c)
                if f == 0 and not (isinstance(G, int) and G < 2):
                    pe.wait_ge(s["y_read"], G - 1)
                g = gs[f % 4]
                w_hi, w_lo = (w2[:, ds(e * 4096 + ((f // 4) * 2048 + part * 1024 + (f % 4) * 256), D)] for part in range(2))
                for t in range(TB):
                    y = ypair[parity][:, t, 0:D]
                    pe.matmul(y, g[:, 0, tile(t)], w_hi, start=f == 0, stop=False)
                    pe.matmul(y, g[:, 0, tile(t)], w_lo, start=False, stop=False)
                    op = pe.matmul(y, g[:, 1, tile(t)], w_hi, start=False, stop=f == FC - 1)
                op.then_inc(s["down_done"], 1)

            def body(G, parity, routed, before):
                def expert_of(n):
                    return pe.value_load(blk_expert[0:1, ds(n, 1)], min_val=0, max_val=E - 1)

                if isinstance(G, int) and G == NSH:
                    pe.wait_ge(s["routed"], 1)
                e = expert_of(G - NSH) if routed else E
                e_before = expert_of(G - (NSH + 1)) if before == "routed" else E
                for f in range(FC):
                    if f == 0:
                        got(pe, "xT_ready", G)
                    up(G, parity, e, f)
                    if f >= 2:
                        down(G, parity, e, f - 2)
                    elif before is not None:
                        down(G - 1, 1 - parity, e_before, FC - 2 + f)
                    if f == 4 and not is_last(G):
                        if next_kind(G, routed) == "routed":
                            pe.wait_ge(s["xrow_loaded"], 16 * (G + (2 - NSH)))
                            transpose_rows(routed_source)
                        else:
                            transpose_rows(shared_source(G + 1))
                if is_last(G):
                    for f in range(FC - 2, FC):
                        down(G, parity, e, f)

            pe.wait_ge(s["xf_ready"], B)
            pe.wait_ge(s["pads_stored"], 16)
            pe.wait_ge(s["k2_ready"], B)
            pe.wait_ge(s["v2_ready"], B)
            pe.wait_ge(s["pT_copied"], B)
            transpose_rows(shared_source(0))
            pe.wait_ge(s["picked_ready"], 1)
            pe.matmul(count_ps[:, 0, :], earlier[:, :], picked, start=True, stop=True)
            pe.matmul(count_ps[:, 1, :], ones16[:, :], picked, start=True, stop=True).then_inc(s["counts_done"], 1)
            pe.wait_ge(s["x2_ready"], B)
            pe.wait_ge(s["logits_copied"], B)
            stream(pe, body)


_INS = ['x', 'ctx_1024', 'L0_attn_W', 'L0_xattn_Wq', 'L0_xattn_bq', 'L0_xattn_Wk', 'L0_xattn_bk', 'L0_xattn_Wv',
        'L0_xattn_bv', 'L0_ffn_Wfc_s', 'L0_ffn_bfc_s', 'L0_ffn_Wproj_s', 'L0_ffn_bproj_s', 'L0_ffn_Wr',
        'L0_ffn_Wfc', 'L0_ffn_bfc', 'L0_ffn_Wproj', 'L0_ffn_bproj']


def kernel(**inputs):
    import numpy as np
    import concourse.bacc as bacc
    from concourse.bass_utils import run_bass_kernel_spmd

    nc = bacc.Bacc("TRN2", target_bir_lowering=False, num_devices=1)
    arrays, args = {}, []
    for name in _INS:
        a = np.ascontiguousarray(inputs[name])
        arrays["in_" + name] = a
        args.append(nc.dram_tensor("in_" + name, a.shape, mybir.dt.from_np(a.dtype), kind="ExternalInput").ap())
    out = nc.dram_tensor("out", inputs["x"].shape, F32, kind="ExternalOutput").ap()
    decoder_layer(nc, *args, out)
    r = run_bass_kernel_spmd(nc, [arrays], core_ids=[0])
    return r.results[0]["out"]
```

```python
from contextlib import ExitStack

import concourse.bass as bass
from concourse import mybir

F32 = mybir.dt.float32
F16 = mybir.dt.float16
I32 = mybir.dt.int32
U32 = mybir.dt.uint32
ALU = mybir.AluOpType
ACT = mybir.ActivationFunctionType
AX = mybir.AxisListType
ds = bass.ds

P = 128
LN_EPS = 1e-5
ATTN_EPS = 1e-6
W_SCALE = 256.0
A_SCALE = 16.0
UNSCALE = 1.0 / (W_SCALE * A_SCALE)
LAG = 4


def decoder_layer(nc, x, ctx_in, attn_w, wq_in, bq_in, wk_in, bk_in, wv_in, bv_in,
                  fc_s, bfc_s, proj_s, bproj_s, wr_in, fc, bfc, proj, bproj, out):
    B, S, D = x.shape
    CK = ctx_in.shape[1]
    E, _, H = fc.shape
    T = B * S
    TB = S // P
    TILES = T // P
    DK = D // P
    FC = H // P
    BLK = S
    NSH = T // BLK
    NRT = 2 * T // BLK + E - 1
    NBLK = NSH + NRT
    ROW = D + E + 1
    HALVES = 2 * (E + 1)
    SCALE = float(D) ** -0.5
    PADS = 3
    PAD_STEPS = NRT // PADS
    assert NRT % PADS == 0 and PAD_STEPS == B - 3
    assert S == 256 and D == 256 and H == 1024 and CK <= P

    rows_dram = nc.dram_tensor("rows_by_expert", [NRT * BLK, ROW], F32).ap()
    x2_dram = nc.dram_tensor("x2_residual", [T, D], F32).ap()

    def tiles_of(ap, b):
        return ap.rearrange("(b t p) n -> b p t n", t=TB, p=P)[ds(b, 1)].rearrange("b p t n -> p (b t) n")

    out_rows = out.rearrange("b s d -> (b s) d")
    x_rows = x.rearrange("b s d -> (b s) d")

    with ExitStack() as stack:
        def sb(name, shape, dt):
            return stack.enter_context(nc.sbuf_tensor(name, shape, dt))

        def pb(name, shape, dt=F32):
            return stack.enter_context(nc.psum_tensor(name, shape, dt))

        def sem(name):
            return stack.enter_context(nc.semaphore(name))

        w1 = sb("w1_parts", [P, HALVES * 2048], F16)
        w2 = sb("w2_parts", [P, HALVES * 2048], F16)
        rows = sb("rows", [P, TILES, ROW], F32)
        rows16 = rows[:, :, :].bitcast(F16)
        rows_i = rows[:, :, :].bitcast(I32)
        stage1 = sb("stage_w1", [P, 1024], F32)
        stage2 = sb("stage_w2", [P, 4, 256], F32)
        ident = sb("ident", [P, P], F32)
        ident16 = sb("ident16", [P, P], F16)
        earlier = sb("earlier", [P, P], F16)
        ones16 = sb("ones16", [P, P], F16)
        NB1 = (E + 1) * FC
        bias_cols = sb("bias_columns", [P, NB1 + 2 * DK], F32)
        bq = bias_cols[:, NB1:NB1 + DK]
        bk = bias_cols[:, NB1 + DK:NB1 + 2 * DK]
        stats = sb("stats", [P, 3, TB, 6], F32)
        mv = sb("mean_var", [P, 3, TB, 2], F32)
        var_eps = sb("var_eps", [P, 3 * TB], F32)
        minus_half = sb("minus_half", [P, 3 * TB], F32)
        carrier = sb("wait_carrier", [P, 1], F32)
        rstd = sb("rstd", [P, 3 * TB], F32)
        nmax = sb("nmax", [P, TB], F32)
        nbias = sb("nbias", [P, TB], F32)
        psum_p = sb("p_sum", [P, TB], F32)
        rinv = sb("rinv", [P, TB], F32)
        zden = sb("z_den", [P, TB], F32)
        zinv = sb("z_inv", [P, TB], F32)
        lg = sb("logits", [P, TB, E], F32)
        max8 = sb("max8", [P, TB, 8], F32)
        max8_at = sb("max8_at", [P, TB, 8], U32)
        top = sb("top_values", [P, TILES, 2], F32)
        top_f = sb("top_experts", [P, TILES, 2], F32)
        dest = sb("dest_rows", [P, 2, TILES], I32)
        blk_expert = sb("block_expert", [P, NRT], I32)

        FW = ROW * TB + 512 + 1024 + 512 + 1024 + 512 + 256
        fbuf = sb("expert_buffers", [P, FW], F32)
        at = [0]

        def cut(n):
            at[0] += n
            return fbuf[:, at[0] - n:at[0]]

        xrow = cut(ROW * TB).rearrange("p (t w) -> p t w", t=TB)
        x2blk = cut(512).rearrange("p (t n) -> p t n", t=TB)
        xT = [cut(512).bitcast(F16).rearrange("p (k l n) -> p k l n", k=DK, l=2) for _ in range(2)]
        g32 = [cut(256) for _ in range(2)]
        gs = [cut(256).bitcast(F16).rearrange("p (l n) -> p l n", l=2) for _ in range(4)]
        ybuf = cut(512).rearrange("p (t n) -> p t n", t=TB)
        b2blk = cut(256)
        gate = [sb(f"gate{i}", [P, TB], F32) for i in range(2)]
        token = [sb(f"token{i}", [P, TB], I32) for i in range(2)]

        last = (HALVES - 6) * 2048
        tail1 = w1[:, last:last + 4 * 2048].bitcast(F32)
        tail2 = w2[:, last:last + 4 * 2048].bitcast(F32)
        regions = [[tail1, 0, 4096], [tail2, 0, 4096], [fbuf, 0, FW]]

        def lend(n, pattern=None, **dims):
            for r in regions:
                if r[2] - r[1] >= n:
                    r[1] += n
                    ap = r[0][:, r[1] - n:r[1]]
                    return ap.rearrange(pattern, **dims) if pattern else ap
            raise ValueError("no room")

        wqkv = lend(DK * 3 * D, "p (k n) -> p k n", k=DK)
        wq = lend(DK * D, "p (k n) -> p k n", k=DK)
        wk = lend(DK * D, "p (k n) -> p k n", k=DK)
        wv = lend(DK * D, "p (k n) -> p k n", k=DK)
        xn = [lend(TB * D, "p (t n) -> p t n", t=TB) for _ in range(3)]
        xnT = [lend(DK * S, "p (k n) -> p k n", k=DK) for _ in range(3)]
        expk = lend(TB * D, "p (t n) -> p t n", t=TB)
        expq = lend(DK * S, "p (k n) -> p k n", k=DK)
        kfeat = lend(TB * D, "p (t n) -> p t n", t=TB)
        qfeatT = lend(DK * S, "p (k n) -> p k n", k=DK)
        q2T = lend(DK * S, "p (k n) -> p k n", k=DK)
        vones = lend(TB * (D + 1), "p (t n) -> p t n", t=TB)
        state = lend(DK * (D + 1), "p (k n) -> p k n", k=DK)
        ctx_sb = lend(D)
        ctxT = lend(DK * CK, "p (k n) -> p k n", k=DK)
        k2T = lend(DK * CK, "p (k n) -> p k n", k=DK)
        v2 = lend(D)
        bv = lend(D)
        prob = lend(TB * CK, "p (t n) -> p t n", t=TB)
        probT = lend(S)
        wr = lend(DK * E, "p (k n) -> p k n", k=DK)
        pad_row = lend(ROW)
        bias_rows = lend(P)

        route = [[tail2, 0, 4096]]

        def scratch(n):
            route[0][1] += n
            return tail2[:, route[0][1] - n:route[0][1]]

        TE = TILES * E

        def te(ap):
            return ap.rearrange("p (t e) -> p t e", e=E)

        hot = [te(scratch(TE)) for _ in range(2)]
        gated = te(scratch(TE))
        picked = scratch(TE).bitcast(F16)[:, 0:TE]
        iota_te = te(scratch(TE))
        iota_i = scratch(TE).bitcast(I32)
        dlog = scratch(TILES)
        edlog = scratch(TILES)
        gden = scratch(TILES)
        g1 = scratch(TILES)
        g2 = scratch(TILES)
        totals = scratch(TE).rearrange("p (e t) -> p e t", e=E)
        keep = scratch(TE).rearrange("p (e t) -> p e t", e=E)
        upto = scratch(TE).rearrange("p (e t) -> p e t", e=E)
        base = scratch(TE).rearrange("p (e t) -> p e t", e=E)
        place = te(scratch(TE))
        chosen = te(scratch(TE))
        dest_f = scratch(2 * TILES).rearrange("p (j t) -> p j t", j=2)
        nblk_i = scratch(E).bitcast(I32)
        nblk_i2 = scratch(E).bitcast(I32)
        nblk = scratch(E)
        ones_e = scratch(E)
        blk_end = scratch(E)
        first_row = scratch(E)
        past = scratch(NRT * E).rearrange("p (n e) -> p n e", e=E)
        iota_blk = scratch(NRT)
        iota_blk_i = scratch(NRT).bitcast(I32)
        blk_f = scratch(NRT)

        bank0 = pb("bank0", [P, 512])
        bank_kv = pb("bank_kv", [P, 2, 512])
        bank3 = pb("bank3", [P, 512])
        bank_st = pb("bank_st", [P, 2, 512])
        bank6 = pb("bank6", [P, 512])
        bank7 = pb("bank7", [P, 512])

        tr = bank0[:, :].rearrange("p (k n) -> p k n", k=DK)
        qps = bank3[:, :].rearrange("p (k n) -> p k n", k=DK)
        q2ps = bank6[:, :].rearrange("p (k n) -> p k n", k=DK)
        ctxT_ps = bank7[:, 0:DK * CK].rearrange("p (k n) -> p k n", k=DK)
        k2T_ps = bank7[:, 256:256 + DK * CK].rearrange("p (k n) -> p k n", k=DK)
        v2_ps = bank7[:, 0:D]
        sc_ps = bank7[:, 0:TB * CK].rearrange("p (t n) -> p t n", t=TB)
        pT_ps = bank7[:, 0:S]
        pv_ps = bank_kv[:, 0, :].rearrange("p (t n) -> p t n", t=TB)
        lg_ps = bank_kv[:, 1, 0:TB * E].rearrange("p (t n) -> p t n", t=TB)
        count_ps = bank6[:, :].rearrange("p (j n) -> p j n", j=2)
        hid = [bank0, bank3]
        ypair = [bank_kv, bank_st]
        rowT_ps = bank7[:, :].bitcast(F16)

        s = {}
        for name in ("wqkv_loaded const_loaded x_loaded ctx_loaded w1_loaded w2_loaded x2_stored pads_stored "
                     "ident16_set ones_set ident_set pow_set biasT_done bias_ready "
                     "sums_step stats_step var_ready rstd_ready xn1_ready xn2_ready xn3_ready "
                     "t1_done t2_done t3_done t1_copied t2_copied t3_copied "
                     "kv_done q_done expk_ready v_copied expq_ready reluk_ready reluq_ready kfeat_ready qfeat_ready "
                     "state_done state_copied attn_done z_step x1_ready "
                     "ctxT_done ctxT_copied k2v2_done k2_ready v2_ready q2_done q2_ready "
                     "scores_done smax_step smax_ready p_ready rinv_ready pT_done pT_copied pv_done x2_ready "
                     "logits_done logits_copied max_step top_step top_ready hi_step xf_ready w_hi w_lo "
                     "route_step route_iota last_hi last_lo exp_gate counts_done picked_ready routed rows_sent "
                     "up_done gelu_done g_hi g_ready down_done y_read y_ready rowT_done xT_ready "
                     "meta_taken carried xrow_loaded x2blk_loaded b2_loaded y_stored y_added").split():
            s[name] = sem(name)

        block = stack.enter_context(nc.Block())

        def live(b):
            return not isinstance(b, int) or 0 <= b < B

        def got(eng, name, b):
            eng.wait_ge(s[name], b + 1)

        def got_if(eng, name, b):
            if isinstance(b, int):
                b = min(b, B - 1)
                if b < 0:
                    return
            eng.wait_ge(s[name], b + 1)

        def apart(eng):
            eng.wait_ge(s["ones_set"], 1)

        def steps(eng, step, first, end):
            for i in range(-2, first):
                step(i)
            with eng.Fori(first, end) as i:
                step(i)
            for i in range(end, B + LAG + 1):
                step(i)

        def half_of(i):
            if isinstance(i, int) and not LAG <= i < B:
                return 2 * E + i if i in (0, 1) else None
            return i - LAG

        def part_count(i):
            if isinstance(i, int) and not LAG <= i < B:
                return min(max(i, 0), 2)
            return i - (LAG - 2)

        def stream(eng, body):
            body(0, 0, False, None)
            body(1, 1, False, "shared")
            with eng.Fori(1, NSH // 2 - 1) as j:
                for c in range(2):
                    body(2 * j + c, c, False, "shared")
            body(NSH - 2, 0, False, "shared")
            body(NSH - 1, 1, False, "shared")
            body(NSH, 0, True, "shared")
            body(NSH + 1, 1, True, "routed")
            with eng.Fori(1, NRT // 2) as j:
                for c in range(2):
                    body(2 * j + (NSH + c), c, True, "routed")
            body(NBLK - 1, 0, True, "routed")

        def is_last(G):
            return isinstance(G, int) and G == NBLK - 1

        def next_kind(G, routed):
            if is_last(G):
                return None
            return "routed" if routed or (isinstance(G, int) and G == NSH - 1) else "shared"

        @block.sync
        def _(sp):
            def load(dst, src):
                sp.dma_start(dst, src).then_inc(s["const_loaded"], 16)

            sp.dma_start(rows[:, 0:TB, 0:D], tiles_of(x_rows, 0)).then_inc(s["x_loaded"], 16)
            sp.dma_start(wqkv, attn_w.rearrange("(k p) n -> p k n", p=P)).then_inc(s["wqkv_loaded"], 16)
            load(wq, wq_in.rearrange("(k p) n -> p k n", p=P))
            load(wk, wk_in.rearrange("(k p) n -> p k n", p=P))
            load(wv, wv_in.rearrange("(k p) n -> p k n", p=P))
            load(wr, wr_in.rearrange("(k p) n -> p k n", p=P))
            load(bias_rows[0:E * FC, :], bfc.rearrange("e (c p) -> (e c) p", p=P))
            load(bias_rows[E * FC:NB1, :], bfc_s.rearrange("(c p) -> c p", p=P))
            load(bias_rows[NB1:NB1 + DK, :], bq_in.rearrange("(k p) -> k p", p=P))
            load(bias_rows[NB1 + DK:NB1 + 2 * DK, :], bk_in.rearrange("(k p) -> k p", p=P))
            load(bv, bv_in.rearrange("(a n) -> a n", a=1).broadcast_to([P, D]))
            w1_half = fc.rearrange("e (k p) f -> (e k) p f", p=P)
            w2_half = proj.rearrange("e (h c p) n -> (e h) p c n", p=P, c=4)
            w1_shared = fc_s.rearrange("(k p) f -> k p f", p=P)
            w2_shared = proj_s.rearrange("(h c p) n -> h p c n", p=P, c=4)

            def load_half(half, before, split="w_lo"):
                shared = isinstance(half, int) and half >= 2 * E
                a = w1_shared[half - 2 * E] if shared else w1_half[ds(half, 1)].rearrange("a p f -> p (a f)")
                c = w2_shared[half - 2 * E] if shared else w2_half[ds(half, 1)].rearrange("a p c n -> p (a c) n")
                sp.wait_ge(s[split], before)
                sp.dma_start(stage1[:, :], a).then_inc(s["w1_loaded"], 16)
                sp.dma_start(stage2[:, :, :], c).then_inc(s["w2_loaded"], 16)

            def step(i):
                if (half := half_of(i)) is not None:
                    load_half(half, part_count(i))
                if not isinstance(i, int) or 1 <= i <= PAD_STEPS:
                    n = i - 1
                    sp.dma_start(rows_dram.rearrange("(n q p) w -> n p q w", p=P, q=PADS * TB)[ds(n, 1)]
                                 .rearrange("n p q w -> p (n q) w"),
                                 pad_row.rearrange("p (q w) -> p q w", q=1).broadcast_to([P, PADS * TB, ROW]))\
                        .then_inc(s["pads_stored"], 16)
                b = i + 3
                if (isinstance(b, int) and 1 <= b < B) or not isinstance(b, int):
                    sp.wait_ge(s["x_loaded"], b * 16)
                    sp.dma_start(rows[:, ds(b * TB, TB), 0:D], tiles_of(x_rows, b)).then_inc(s["x_loaded"], 16)
                if live(i - 1):
                    b = i - 1
                    sp.wait_ge(s["ctxT_done"], b)
                    sp.dma_start(ctx_sb[0:CK, :], ctx_in[ds(b, 1)].rearrange("b s d -> s (b d)"))\
                        .then_inc(s["ctx_loaded"], 16)
                if live(i - 3):
                    b = i - 3
                    got(sp, "x2_ready", b)
                    sp.wait_ge(s["x2_stored"], b * 16)
                    sp.dma_start(tiles_of(x2_dram, b), rows[:, ds(b * TB, TB), 0:D])\
                        .then_inc(s["x2_stored"], 16)

            sp.wait_ge(s["pow_set"], 4)
            steps(sp, step, LAG, B - 3)

            sp.wait_ge(s["logits_done"], B)
            sp.wait_ge(s["pads_stored"], PAD_STEPS * 16)

            def load_b2(G, e):
                sp.wait_ge(s["y_read"], G)
                src = bproj_s.rearrange("(a n) -> a n", a=1) if isinstance(e, int) else bproj[ds(e, 1)]
                sp.dma_start(b2blk, src.broadcast_to([P, D])).then_inc(s["b2_loaded"], 16)

            def finish_shared(G):
                got(sp, "y_ready", G)
                sp.dma_start(tiles_of(out_rows, G), ybuf).then_inc(s["y_stored"], 16)

            def shared_block(G):
                if isinstance(G, int) and G == 0:
                    sp.wait_ge(s["x2_stored"], B * 16)
                else:
                    sp.wait_ge(s["y_ready"], G)
                sp.dma_start(x2blk, tiles_of(x2_dram, G)).then_inc(s["x2blk_loaded"], 16)
                load_b2(G, E)
                if not (isinstance(G, int) and G == 0):
                    finish_shared(G - 1)

            def last_half(q):
                load_half(2 * E - 4 + q, q, split="last_lo")

            for G in range(3):
                shared_block(G)
            sp.wait_ge(s["w_lo"], HALVES - 4)
            sp.wait_ge(s["routed"], 1)
            last_half(0)
            with sp.Fori(1, NSH // 4) as j:
                for c in range(2):
                    shared_block(2 * j + (1 + c))
            for q in range(1, 4):
                last_half(q)
                for c in range(2):
                    shared_block(NSH // 2 + 2 * q - 1 + c)
            sp.wait_ge(s["rows_sent"], 2 * TILES * 16)

            def load_rows(n):
                sp.wait_ge(s["meta_taken"], n)
                sp.dma_start(xrow, tiles_of(rows_dram, n)).then_inc(s["xrow_loaded"], 16)

            def expert_of(n):
                return sp.value_load(blk_expert[0:1, ds(n, 1)], min_val=0, max_val=E - 1)

            load_rows(0)
            shared_block(NSH - 1)
            load_rows(1)
            load_b2(NSH, expert_of(0))
            finish_shared(NSH - 1)
            with sp.Fori(1, NRT - 1) as n:
                load_rows(n + 1)
                load_b2(n + NSH, expert_of(n))
            load_b2(NRT - 1 + NSH, expert_of(NRT - 1))

        @block.gpsimd
        def _(pool):
            pool.memset(minus_half[:, :], -0.5)
            pool.memset(pad_row, 0.0).then_inc(s["pow_set"], 1)
            pool.memset(ident[:, :], 0.0).then_inc(s["pow_set"], 1)
            pool.memset(earlier[:, :], 1.0).then_inc(s["pow_set"], 1)
            pool.wait_ge(s["pow_set"], 2)
            pool.affine_select(out=ident[:, :], in_=ident[:, :], compare_op=ALU.not_equal, fill=1.0,
                               base=0, pattern=[[-1, P]], channel_multiplier=1).then_inc(s["ident_set"], 1)
            pool.memset(pad_row.bitcast(I32)[:, ROW - 1:ROW], T).then_inc(s["pow_set"], 1)
            pool.wait_ge(s["pow_set"], 3)
            pool.affine_select(out=earlier[:, :], in_=earlier[:, :], compare_op=ALU.is_gt, fill=0.0,
                               base=0, pattern=[[1, P]], channel_multiplier=-1).then_inc(s["ident_set"], 1)
            pool.wait_ge(s["ident_set"], 1)
            pool.tensor_copy(ident16[:, :], ident[:, :]).then_inc(s["ident16_set"], 1)

            def step(k):
                pool.wait_ge(s["var_ready"], k + 1)
                pool.tensor_tensor(rstd[:, :], var_eps[:, :], minus_half[:, :], ALU.pow).then_inc(s["rstd_ready"], 1)

            with pool.Fori(0, B + LAG + 1) as k:
                step(k)

            pool.wait_ge(s["logits_done"], B)
            pool.wait_ge(s["xf_ready"], B)
            pool.iota(iota_i, [[0, TILES], [1, E]], base=0, channel_multiplier=0).then_inc(s["route_iota"], 1)
            pool.iota(iota_blk_i, [[1, NRT]], base=0, channel_multiplier=0).then_inc(s["route_iota"], 1)
            pool.memset(keep, 1.0).then_inc(s["route_iota"], 1)
            pool.memset(ones_e, 1.0)
            pool.wait_ge(s["route_iota"], 3)
            pool.memset(keep[:, :, 0:1], 0.0).then_inc(s["route_iota"], 1)
            pool.iota(rows_i[:, :, ROW - 1], [[P, TILES]], base=0, channel_multiplier=1)\
                .then_inc(s["route_iota"], 1)

            pool.wait_ge(s["route_iota"], 5)
            pool.wait_ge(s["routed"], 1)
            pool.wait_ge(s["pads_stored"], PAD_STEPS * 16)
            for t in range(TILES):
                for j in range(2):
                    pool.indirect_dma_start(
                        out=rows_dram, out_offset=bass.IndirectOffsetOnAxis(ap=dest[:, j, t:t + 1].bitcast(U32), axis=0),
                        in_=rows[:, t, :], in_offset=None).then_inc(s["rows_sent"], 16)

            for q in range(4):
                half = 2 * E - 4 + q
                parts = ((w1, stage1[:, :]), (w2, stage2[:, :, :].rearrange("p c n -> p (c n)")))
                pool.wait_ge(s["w1_loaded"], (HALVES - 3 + q) * 16)
                pool.wait_ge(s["w2_loaded"], (HALVES - 3 + q) * 16)
                for w, stage in parts:
                    op = pool.tensor_scalar(stage, stage, W_SCALE, None, ALU.mult)
                op.then_inc(s["last_hi"], 1)
                pool.wait_ge(s["last_hi"], 2 * q + 1)
                for w, stage in parts:
                    op = pool.tensor_copy(w[:, half * 2048:half * 2048 + 1024], stage)
                op.then_inc(s["last_hi"], 1)
                pool.wait_ge(s["last_hi"], 2 * q + 2)
                for w, stage in parts:
                    op = pool.tensor_tensor(w[:, half * 2048 + 1024:half * 2048 + 2048], stage,
                                            w[:, half * 2048:half * 2048 + 1024], ALU.subtract)
                op.then_inc(s["last_lo"], 1)

            last_token = pool.to_reg(T - 1)

            def add_block(n, parity):
                pool.wait_ge(s["y_ready"], n + (NSH + 1))
                pool.wait_ge(s["carried"], n)
                if isinstance(n, int) and n == 0:
                    pool.wait_ge(s["y_stored"], NSH * 16)
                else:
                    pool.wait_ge(s["y_added"], n * (16 * TB))
                pool.tensor_tensor(carrier[:, :], minus_half[:, 0:1], minus_half[:, 0:1], ALU.add)\
                    .then_inc(s["carried"], 1)
                for t in range(TB):
                    pool.indirect_dma_start(
                        out=out_rows, out_offset=bass.IndirectOffsetOnAxis(ap=token[parity][:, t:t + 1].bitcast(U32), axis=0),
                        in_=ybuf[:, t, :], in_offset=None, bounds_check=last_token, oob_is_err=False,
                        compute_op=ALU.add).then_inc(s["y_added"], 16)

            add_block(0, 0)
            with pool.Fori(0, (NRT - 1) // 2) as j:
                for c in range(2):
                    add_block(2 * j + (1 + c), (1 + c) % 2)
            pool.wait_ge(s["y_added"], NRT * TB * 16)

        @block.scalar
        def _(act):
            def copy(dst, src, name):
                act.activation(dst, src, ACT.Copy).then_inc(s[name], 1)

            def convert_hi(half, before):
                act.wait_ge(s["w1_loaded"], (before + 1) * 16)
                act.wait_ge(s["w2_loaded"], (before + 1) * 16)
                act.activation(w1[:, ds(half * 2048, 1024)], stage1[:, :], ACT.Copy, scale=W_SCALE)
                act.activation(w2[:, ds(half * 2048, 1024)], stage2[:, :, :].rearrange("p c n -> p (c n)"),
                               ACT.Copy, scale=W_SCALE).then_inc(s["w_hi"], 1)

            def step(i):
                if live(i):
                    got(act, "t1_done", i)
                    copy(xnT[0], tr, "t1_copied")
                if live(i - 1):
                    got(act, "state_done", i - 1)
                    copy(state, bank_st[:, :, 0:D + 1], "state_copied")
                if live(i - 3):
                    b = i - 3
                    got(act, "smax_ready", b)
                    got_if(act, "pT_done", b - 1)
                    for t in range(TB):
                        op = act.activation(prob[:, t, :], sc_ps[:, t, :], ACT.Exp, bias=nbias[:, t:t + 1],
                                            scale=SCALE, accum_out=psum_p[:, t:t + 1])
                    op.then_inc(s["p_ready"], 1)
                if (half := half_of(i)) is not None:
                    convert_hi(half, part_count(i))
                if live(i):
                    got(act, "kv_done", i)
                    got_if(act, "kfeat_ready", i - 1)
                    act.activation(expk, bank_kv[:, :, 0:D], ACT.Exp).then_inc(s["expk_ready"], 1)
                    got_if(act, "state_done", i - 1)
                    act.activation(kfeat, bank_kv[:, :, 0:D], ACT.Relu).then_inc(s["reluk_ready"], 1)
                    copy(vones[:, :, 0:D], bank_kv[:, :, D:2 * D], "v_copied")
                    got(act, "q_done", i)
                    got_if(act, "qfeat_ready", i - 1)
                    act.activation(expq, qps, ACT.Exp).then_inc(s["expq_ready"], 1)
                if live(i - 3):
                    got(act, "pT_done", i - 3)
                    got_if(act, "pv_done", i - 4)
                    copy(probT[0:CK, :], pT_ps[0:CK, :], "pT_copied")
                if live(i - 2):
                    got(act, "t2_done", i - 2)
                    copy(xnT[1], tr, "t2_copied")
                if live(i):
                    got_if(act, "attn_done", i - 1)
                    act.activation(qfeatT, qps, ACT.Relu).then_inc(s["reluq_ready"], 1)
                if live(i - 2):
                    got(act, "ctxT_done", i - 2)
                    copy(ctxT, ctxT_ps, "ctxT_copied")
                if live(i - 4):
                    got(act, "t3_done", i - 4)
                    copy(xnT[2], tr, "t3_copied")
                if isinstance(i, int) and i == 0:
                    act.wait_ge(s["biasT_done"], 1)
                    copy(bias_cols[:, :], bank6[:, 0:NB1 + 2 * DK], "bias_ready")
                    act.wait_ge(s["bias_ready"], 1)
                if live(i - 2):
                    got(act, "k2v2_done", i - 2)
                    for m in range(DK):
                        op = act.activation(k2T[:, m, :], k2T_ps[:, m, :], ACT.Identity, bias=bk[:, m:m + 1])
                    op.then_inc(s["k2_ready"], 1)
                    got(act, "q2_done", i - 2)
                    for m in range(DK):
                        op = act.activation(q2T[:, m, :], q2ps[:, m, :], ACT.Identity, bias=bq[:, m:m + 1])
                    op.then_inc(s["q2_ready"], 1)

            steps(act, step, LAG + 1, B)

            act.wait_ge(s["route_step"], 1)
            act.activation(edlog, dlog, ACT.Exp).then_inc(s["exp_gate"], 1)

            def body(G, parity, routed, before):
                e = E
                if routed:
                    e = act.value_load(blk_expert[0:1, ds(G - NSH, 1)], min_val=0, max_val=E - 1)
                for f in range(FC):
                    got(act, "up_done", FC * G + f)
                    if not (isinstance(G, int) and FC * G + f < 2):
                        act.wait_ge(s["g_ready"], FC * G + (f - 1))
                    bias = bias_cols[:, ds(e * FC + f, 1)]
                    act.activation(g32[f % 2], hid[f % 2][:, 0:BLK], ACT.Gelu_apprx_tanh, bias=bias,
                                   scale=UNSCALE).then_inc(s["gelu_done"], 1)
                    if f == 5 and not is_last(G):
                        got(act, "rowT_done", G + 1)
                        copy(xT[1 - parity].rearrange("p k l n -> p (k l n)"), rowT_ps, "xT_ready")

            act.wait_ge(s["logits_done"], B)
            got(act, "rowT_done", 0)
            copy(xT[0].rearrange("p k l n -> p (k l n)"), rowT_ps, "xT_ready")
            stream(act, body)

        @block.vector
        def _(dve):
            route_count = [0]

            def chain(op, name, count, own=False):
                op.then_inc(s[name], 1)
                if own:
                    apart(dve)
                dve.wait_ge(s[name], count)

            def convert_lo(half, before):
                dve.wait_ge(s["w_hi"], before + 1)
                for w, stage in ((w1, stage1[:, :]), (w2, stage2[:, :, :].rearrange("p c n -> p (c n)"))):
                    op = dve.scalar_tensor_tensor(w[:, ds(half * 2048 + 1024, 1024)], stage, W_SCALE,
                                                  w[:, ds(half * 2048, 1024)], ALU.mult, ALU.subtract)
                op.then_inc(s["w_lo"], 1)

            def layer_norm(n, b):
                got_if(dve, f"t{n + 1}_done", b - 1)
                if n == 2:
                    got_if(dve, "xf_ready", b - 1)
                for t in range(TB):
                    r = rows[:, ds(b * TB + t, 1), 0:D].rearrange("p a n -> p (a n)")
                    op = dve.tensor_scalar(xn[n][:, t, :], r, mv[:, n, t, 0:1],
                                           rstd[:, n * TB + t:n * TB + t + 1], ALU.subtract, ALU.mult)
                op.then_inc(s[f"xn{n + 1}_ready"], 1)

            def step(i):
                if live(i - 5):
                    got(dve, "logits_done", i - 5)
                    dve.tensor_copy(lg[:, :, :], lg_ps).then_inc(s["logits_copied"], 1)
                if live(i + 1) or live(i - 2) or live(i - 4):
                    dve.wait_ge(s["rstd_ready"], i + 2)
                for n, b in ((1, i - 2), (2, i - 4), (0, i + 1)):
                    if live(b):
                        layer_norm(n, b)
                if live(i - 3):
                    b = i - 3
                    got(dve, "scores_done", b)
                    got_if(dve, "p_ready", b - 1)
                    chain(dve.reduce_max(nmax[:, :], sc_ps, AX.X, negate=True), "smax_step", b + 1)
                    dve.tensor_scalar(nbias[:, :], nmax[:, :], SCALE, None, ALU.mult).then_inc(s["smax_ready"], 1)
                if live(i - 4):
                    b = i - 4
                    dve.wait_ge(s["x2_stored"], (b + 1) * 16)
                    got(dve, "xn3_ready", b)
                    hi = rows16[:, ds(b * TB, TB), 0:D]
                    lo = rows16[:, ds(b * TB, TB), D:2 * D]
                    chain(dve.tensor_scalar(hi, xn[2], A_SCALE, None, ALU.mult), "hi_step", b + 1)
                    dve.scalar_tensor_tensor(lo, xn[2], A_SCALE, hi, ALU.mult, ALU.subtract).then_inc(s["xf_ready"], 1)
                if live(i - 5):
                    b = i - 5
                    apart(dve)
                    got(dve, "logits_copied", b)
                    for t in range(TB):
                        op = dve.max(max8[:, t, :], lg[:, t, :])
                    chain(op, "max_step", b + 1, own=True)
                    for t in range(TB):
                        op = dve.max_index(max8_at[:, t, :], max8[:, t, :], lg[:, t, :])
                    chain(op, "top_step", b + 1)
                    dve.tensor_copy(top[:, ds(b * TB, TB), :], max8[:, :, 0:2])
                    dve.tensor_copy(top_f[:, ds(b * TB, TB), :], max8_at[:, :, 0:2]).then_inc(s["top_ready"], 1)
                if (half := half_of(i)) is not None:
                    convert_lo(half, part_count(i))
                if live(i):
                    got(dve, "reluk_ready", i)
                    dve.scalar_tensor_tensor(kfeat, expk, 1.0, kfeat, ALU.min, ALU.add).then_inc(s["kfeat_ready"], 1)
                if live(i - 3):
                    got(dve, "p_ready", i - 3)
                    dve.reciprocal(rinv[:, :], psum_p[:, :]).then_inc(s["rinv_ready"], 1)
                if live(i - 1):
                    b = i - 1
                    got(dve, "attn_done", b)
                    chain(dve.tensor_scalar(zden[:, :], bank_st[:, :, D], ATTN_EPS, None, ALU.add),
                          "z_step", 2 * b + 1)
                    chain(dve.reciprocal(zinv[:, :], zden[:, :]), "z_step", 2 * b + 2)
                    for t in range(TB):
                        r = rows[:, ds(b * TB + t, 1), 0:D].rearrange("p a n -> p (a n)")
                        op = dve.scalar_tensor_tensor(r, bank_st[:, t, 0:D], zinv[:, t:t + 1], r, ALU.mult, ALU.add)
                    op.then_inc(s["x1_ready"], 1)
                if live(i):
                    got(dve, "reluq_ready", i)
                    dve.scalar_tensor_tensor(qfeatT, expq, 1.0, qfeatT, ALU.min, ALU.add).then_inc(s["qfeat_ready"], 1)
                if live(i - 3):
                    b = i - 3
                    got(dve, "rinv_ready", b)
                    got(dve, "pv_done", b)
                    for t in range(TB):
                        r = rows[:, ds(b * TB + t, 1), 0:D].rearrange("p a n -> p (a n)")
                        op = dve.scalar_tensor_tensor(r, pv_ps[:, t, :], rinv[:, t:t + 1], r, ALU.mult, ALU.add)
                    op.then_inc(s["x2_ready"], 1)

                norms = [(n, b) for n, b in ((0, i + 2), (1, i - 1), (2, i - 3)) if live(b)]
                if norms:
                    for n, b in norms:
                        apart(dve)
                        if n == 0:
                            dve.wait_ge(s["x_loaded"], (b + 1) * 16)
                        else:
                            got(dve, "x1_ready" if n == 1 else "x2_ready", b)
                        for t in range(TB):
                            r = rows[:, ds(b * TB + t, 1), 0:D].rearrange("p a n -> p (a n)")
                            op = dve.bn_stats(stats[:, n, t, :], r)
                    chain(op, "sums_step", i + 3, own=True)
                    for n, b in norms:
                        for t in range(TB):
                            op = dve.bn_aggr(mv[:, n, t, :], stats[:, n, t, :])
                    chain(op, "stats_step", i + 3)
                    dve.tensor_scalar(var_eps[:, :].rearrange("p (n t) -> p n t", n=3), mv[:, :, :, 1], LN_EPS, None,
                                      ALU.add).then_inc(s["var_ready"], 1)
                if live(i - 2):
                    b = i - 2
                    got(dve, "k2_ready", b)
                    dve.tensor_tensor(v2[0:CK, :], v2_ps[0:CK, :], bv[0:CK, :], ALU.add).then_inc(s["v2_ready"], 1)

            dve.memset(mv[:, :, :, :], 1.0)
            dve.memset(vones[:, :, D:D + 1], 1.0)
            dve.memset(ones16[:, :], 1.0).then_inc(s["ones_set"], 1)
            dve.wait_ge(s["ones_set"], 1)
            steps(dve, step, LAG + 2, B - 2)

            def then(op):
                route_count[0] += 1
                chain(op, "route_step", route_count[0])

            def over_e(ap):
                return ap.rearrange("p (t a) -> p t a", a=1).broadcast_to([P, TILES, E])

            dve.wait_ge(s["top_ready"], B)
            dve.wait_ge(s["w_lo"], 2 + B - LAG)
            then(dve.tensor_tensor(dlog, top[:, :, 1], top[:, :, 0], ALU.subtract))
            dve.wait_ge(s["route_iota"], 4)
            dve.tensor_copy(iota_te.rearrange("p t e -> p (t e)"), iota_i)
            then(dve.tensor_copy(iota_blk, iota_blk_i))
            for j in range(2):
                op = dve.tensor_tensor(hot[j], iota_te, top_f[:, :, j:j + 1].broadcast_to([P, TILES, E]), ALU.is_equal)
            then(op)
            dve.tensor_tensor(picked.rearrange("p (t e) -> p t e", e=E), hot[0], hot[1], ALU.add)\
                .then_inc(s["picked_ready"], 1)
            def route(part):
                if part == 0:
                    dve.wait_ge(s["exp_gate"], 1)
                    then(dve.tensor_scalar(gden, edlog, 1.0, None, ALU.add))
                    then(dve.reciprocal(g1, gden))
                elif part == 1:
                    then(dve.tensor_tensor(g2, g1, edlog, ALU.mult))
                    dve.tensor_tensor(gated, hot[0], over_e(g1), ALU.mult)
                elif part == 2:
                    then(dve.tensor_tensor(chosen, hot[1], over_e(g2), ALU.mult))
                    then(dve.tensor_tensor(rows[:, :, D:D + E], gated, chosen, ALU.add))
                elif part == 3:
                    dve.wait_ge(s["counts_done"], 1)
                    then(dve.tensor_copy(totals, count_ps[:, 1, :].rearrange("p (t e) -> p e t", e=E)))
                elif part == 4:
                    then(dve.tensor_tensor_scan(upto.rearrange("p e t -> p (e t)"), keep.rearrange("p e t -> p (e t)"),
                                                totals.rearrange("p e t -> p (e t)"), 0.0, ALU.mult, ALU.add))
                elif part == 5:
                    then(dve.tensor_scalar(nblk_i, upto[:, :, TILES - 1], float(BLK - 1), None, ALU.add))
                    then(dve.tensor_scalar(nblk_i2, nblk_i, BLK.bit_length() - 1, None, ALU.logical_shift_right))
                    then(dve.tensor_copy(nblk, nblk_i2))
                elif part == 6:
                    then(dve.tensor_tensor_scan(blk_end, ones_e, nblk, 0.0, ALU.mult, ALU.add))
                    then(dve.tensor_tensor(first_row, blk_end, nblk, ALU.subtract))
                elif part == 7:
                    dve.tensor_tensor(base, upto, totals, ALU.subtract)
                elif part == 8:
                    then(dve.tensor_tensor(past, iota_blk.rearrange("p (n a) -> p n a", a=1).broadcast_to([P, NRT, E]),
                                           blk_end.rearrange("p (a e) -> p a e", a=1).broadcast_to([P, NRT, E]),
                                           ALU.is_ge))
                elif part == 9:
                    then(dve.tensor_reduce(blk_f, past, AX.X, ALU.add))
                    dve.tensor_scalar(blk_expert[:, :], blk_f, float(E - 1), None, ALU.min)
                elif part == 10:
                    then(dve.scalar_tensor_tensor(
                        base, first_row.rearrange("p (e a) -> p e a", a=1).broadcast_to([P, E, TILES]), float(BLK),
                        base, ALU.mult, ALU.add))
                elif part == 11:
                    then(dve.tensor_tensor(place, te(count_ps[:, 0, :]), base.rearrange("p e t -> p t e"), ALU.add))
                elif part < 16:
                    j = (part - 12) // 2
                    if part % 2 == 0:
                        then(dve.tensor_tensor(chosen, place, hot[j], ALU.mult))
                    else:
                        then(dve.tensor_reduce(dest_f[:, j, :], chosen, AX.X, ALU.add))
                    if part == 15:
                        dve.tensor_copy(dest[:, :, :], dest_f).then_inc(s["routed"], 1)

            def evacuate(G, parity, shared):
                dve.wait_ge(s["down_done"], FC * (G + 1))
                dve.wait_ge(s["b2_loaded"], 16 * (G + 1))
                if not (isinstance(G, int) and G == 0):
                    if shared or (isinstance(G, int) and G == NSH):
                        dve.wait_ge(s["y_stored"], 16 * G)
                    else:
                        dve.wait_ge(s["y_added"], (16 * TB) * (G - NSH))
                for t in range(TB):
                    op = dve.scalar_tensor_tensor(ybuf[:, t, :], ypair[parity][:, t, 0:D], UNSCALE, b2blk,
                                                  ALU.mult, ALU.add)
                op.then_inc(s["y_read"], 1)
                dve.wait_ge(s["y_read"], G + 1)
                if shared:
                    dve.wait_ge(s["x2blk_loaded"], 16 * (G + 1))
                    dve.tensor_tensor(ybuf, ybuf, x2blk, ALU.add).then_inc(s["y_ready"], 1)
                else:
                    for t in range(TB):
                        op = dve.tensor_scalar(ybuf[:, t, :], ybuf[:, t, :], gate[parity][:, t:t + 1], None, ALU.mult)
                    op.then_inc(s["y_ready"], 1)

            def body(G, parity, routed, before):
                for f in range(FC):
                    c = FC * G + f
                    got(dve, "gelu_done", c)
                    if not (isinstance(c, int) and c < 4):
                        dve.wait_ge(s["down_done"], c - 3)
                    g = gs[f % 4]
                    chain(dve.tensor_scalar(g[:, 0, :], g32[f % 2], A_SCALE, None, ALU.mult), "g_hi", c + 1)
                    dve.scalar_tensor_tensor(g[:, 1, :], g32[f % 2], A_SCALE, g[:, 0, :], ALU.mult, ALU.subtract)\
                        .then_inc(s["g_ready"], 1)
                    if isinstance(G, int) and G < 2:
                        route(FC * G + f)
                    if f == 2 and not (isinstance(G, int) and G == 0):
                        evacuate(G - 1, 1 - parity, shared=before == "shared")
                    if f == 6 and next_kind(G, routed) == "routed":
                        n = G + (1 - NSH)
                        expert = dve.value_load(blk_expert[0:1, ds(n, 1)], min_val=0, max_val=E - 1)
                        got(dve, "rowT_done", G + 1)
                        if not (isinstance(n, int) and n < 2):
                            dve.wait_ge(s["y_added"], (n - 1) * (16 * TB))
                        dve.tensor_copy(gate[1 - parity][:, :],
                                        xrow[:, :, ds(expert + D, 1)].rearrange("p t a -> p (t a)"))
                        dve.tensor_copy(token[1 - parity][:, :], xrow[:, :, ROW - 1].bitcast(I32))\
                            .then_inc(s["meta_taken"], 1)

            dve.wait_ge(s["xf_ready"], B)
            stream(dve, body)
            evacuate(NBLK - 1, 0, shared=False)

        @block.tensor
        def _(pe):
            def tile(t):
                return slice(t * P, (t + 1) * P)

            def transpose_norm(n):
                for t in range(TB):
                    for k in range(DK):
                        op = pe.transpose(tr[:, k, tile(t)], xn[n][:, t, tile(k)], ident[:, :])
                return op

            def step(i):
                if live(i):
                    got(pe, "xn1_ready", i)
                    got_if(pe, "t3_copied", i - 5)
                    transpose_norm(0).then_inc(s["t1_done"], 1)
                if live(i - 1):
                    b = i - 1
                    got(pe, "kfeat_ready", b)
                    got(pe, "v_copied", b)
                    got_if(pe, "x1_ready", b - 1)
                    for m in range(DK):
                        for t in range(TB):
                            op = pe.matmul(bank_st[:, m, 0:D + 1], kfeat[:, t, tile(m)], vones[:, t, :],
                                           start=t == 0, stop=t == TB - 1)
                    op.then_inc(s["state_done"], 1)
                if live(i - 3):
                    b = i - 3
                    got(pe, "q2_ready", b)
                    got(pe, "v2_ready", b)
                    for t in range(TB):
                        for m in range(DK):
                            op = pe.matmul(sc_ps[:, t, :], q2T[:, m, tile(t)], k2T[:, m, :], start=m == 0, stop=m == DK - 1)
                    op.then_inc(s["scores_done"], 1)
                if live(i):
                    if isinstance(i, int) and i == 0:
                        pe.wait_ge(s["wqkv_loaded"], 16)
                    got(pe, "t1_copied", i)
                    got_if(pe, "x2_ready", i - 4)
                    got_if(pe, "logits_copied", i - 5)
                    for t in range(TB):
                        for k in range(DK):
                            op = pe.matmul(bank_kv[:, t, :], xnT[0][:, k, tile(t)], wqkv[:, k, D:3 * D],
                                           start=k == 0, stop=k == DK - 1)
                    op.then_inc(s["kv_done"], 1)
                    got_if(pe, "reluq_ready", i - 1)
                    for m in range(DK):
                        for k in range(DK):
                            op = pe.matmul(qps[:, m, :], wqkv[:, k, tile(m)], xnT[0][:, k, :],
                                           start=k == 0, stop=k == DK - 1)
                    op.then_inc(s["q_done"], 1)
                if isinstance(i, int) and i == 0:
                    pe.wait_ge(s["const_loaded"], 9 * 16)
                    n = NB1 + 2 * DK
                    pe.transpose(bank6[:, 0:n], bias_rows[0:n, :], ident[0:n, 0:n]).then_inc(s["biasT_done"], 1)
                if live(i - 3):
                    got(pe, "p_ready", i - 3)
                    for t in range(TB):
                        op = pe.transpose(pT_ps[0:CK, tile(t)], prob[:, t, :], ident[:, :])
                    op.then_inc(s["pT_done"], 1)
                if live(i - 2):
                    got(pe, "xn2_ready", i - 2)
                    got_if(pe, "t1_copied", i)
                    transpose_norm(1).then_inc(s["t2_done"], 1)
                if live(i - 1):
                    b = i - 1
                    got(pe, "state_copied", b)
                    got(pe, "qfeat_ready", b)
                    for t in range(TB):
                        for m in range(DK):
                            op = pe.matmul(bank_st[:, t, 0:D + 1], qfeatT[:, m, tile(t)], state[:, m, :],
                                           start=m == 0, stop=m == DK - 1)
                    op.then_inc(s["attn_done"], 1)
                if live(i - 2):
                    b = i - 2
                    pe.wait_ge(s["ctx_loaded"], (b + 1) * 16)
                    got_if(pe, "pT_copied", b - 1)
                    for k in range(DK):
                        op = pe.transpose(ctxT_ps[:, k, :], ctx_sb[0:CK, tile(k)], ident[0:CK, 0:CK])
                    op.then_inc(s["ctxT_done"], 1)
                if live(i - 3):
                    b = i - 3
                    got(pe, "pT_copied", b)
                    got_if(pe, "v_copied", i)
                    for t in range(TB):
                        op = pe.matmul(pv_ps[:, t, :], probT[0:CK, tile(t)], v2[0:CK, :], start=True, stop=True)
                    op.then_inc(s["pv_done"], 1)
                if live(i - 4):
                    got(pe, "xn3_ready", i - 4)
                    got_if(pe, "t2_copied", i - 2)
                    transpose_norm(2).then_inc(s["t3_done"], 1)
                if live(i - 2):
                    b = i - 2
                    got(pe, "ctxT_copied", b)
                    for m in range(DK):
                        for k in range(DK):
                            pe.matmul(k2T_ps[:, m, :], wk[:, k, tile(m)], ctxT[:, k, :], start=k == 0, stop=k == DK - 1)
                    for k in range(DK):
                        op = pe.matmul(v2_ps[0:CK, :], ctxT[:, k, :], wv[:, k, :], start=k == 0, stop=k == DK - 1)
                    op.then_inc(s["k2v2_done"], 1)
                    got(pe, "t2_copied", b)
                    if isinstance(b, int) and b == 0:
                        pe.wait_ge(s["bias_ready"], 1)
                    got_if(pe, "q2_ready", b - 1)
                    for m in range(DK):
                        for k in range(DK):
                            op = pe.matmul(q2ps[:, m, :], wq[:, k, tile(m)], xnT[1][:, k, :], start=k == 0, stop=k == DK - 1)
                    op.then_inc(s["q2_done"], 1)
                if live(i - 4):
                    got(pe, "t3_copied", i - 4)
                    got_if(pe, "v_copied", i)
                    for t in range(TB):
                        for k in range(DK):
                            op = pe.matmul(lg_ps[:, t, :], xnT[2][:, k, tile(t)], wr[:, k, :], start=k == 0, stop=k == DK - 1)
                    op.then_inc(s["logits_done"], 1)

            pe.wait_ge(s["ident_set"], 1)
            steps(pe, step, LAG + 1, B)

            def transpose_rows(source):
                for k in range(DK):
                    for part in range(2):
                        for t in range(TB):
                            at = ((k * 2 + part) * TB + t) * P
                            op = pe.transpose(rowT_ps[:, at:at + P], source(t, part, k), ident16[:, :])
                op.then_inc(s["rowT_done"], 1)

            def shared_source(G):
                def source(t, part, k):
                    at = part * D + k * P
                    return rows16[:, ds(G * TB + t, 1), at:at + P].rearrange("p a n -> p (a n)")
                return source

            xrow16 = xrow.bitcast(F16)

            def routed_source(t, part, k):
                at = part * D + k * P
                return xrow16[:, t, at:at + P]

            def up(G, parity, e, f):
                c = FC * G + f
                if not (isinstance(c, int) and c < 2):
                    pe.wait_ge(s["gelu_done"], c - 1)
                x = xT[parity]
                for k in range(DK):
                    w_hi, w_lo = (w1[:, ds(e * 4096 + (k * 2048 + part * 1024 + f * P), P)] for part in range(2))
                    pe.matmul(hid[f % 2][:, 0:BLK], w_hi, x[:, k, 0, :], start=k == 0, stop=False)
                    pe.matmul(hid[f % 2][:, 0:BLK], w_hi, x[:, k, 1, :], start=False, stop=False)
                    op = pe.matmul(hid[f % 2][:, 0:BLK], w_lo, x[:, k, 0, :], start=False, stop=k == DK - 1)
                op.then_inc(s["up_done"], 1)

            def down(G, parity, e, f):
                c = FC * G + f
                got(pe, "g_ready", c)
                if f == 0 and not (isinstance(G, int) and G < 2):
                    pe.wait_ge(s["y_read"], G - 1)
                g = gs[f % 4]
                w_hi, w_lo = (w2[:, ds(e * 4096 + ((f // 4) * 2048 + part * 1024 + (f % 4) * 256), D)] for part in range(2))
                for t in range(TB):
                    y = ypair[parity][:, t, 0:D]
                    pe.matmul(y, g[:, 0, tile(t)], w_hi, start=f == 0, stop=False)
                    pe.matmul(y, g[:, 0, tile(t)], w_lo, start=False, stop=False)
                    op = pe.matmul(y, g[:, 1, tile(t)], w_hi, start=False, stop=f == FC - 1)
                op.then_inc(s["down_done"], 1)

            held = [E]

            def body(G, parity, routed, before):
                def expert_of(n):
                    return pe.value_load(blk_expert[0:1, ds(n, 1)], min_val=0, max_val=E - 1)

                if isinstance(G, int) and G == NSH:
                    pe.wait_ge(s["routed"], 1)
                    pe.wait_ge(s["last_lo"], 4)
                e = expert_of(G - NSH) if routed else E
                if parity == 1:
                    e_before = held[0]
                else:
                    e_before = expert_of(G - (NSH + 1)) if before == "routed" else E
                held[0] = e
                for f in range(FC):
                    if f == 0:
                        got(pe, "xT_ready", G)
                    up(G, parity, e, f)
                    if f >= 2:
                        down(G, parity, e, f - 2)
                    elif before is not None:
                        down(G - 1, 1 - parity, e_before, FC - 2 + f)
                    if f == 1 and isinstance(G, int) and G == 0:
                        pe.wait_ge(s["picked_ready"], 1)
                        pe.matmul(count_ps[:, 0, :], earlier[:, :], picked, start=True, stop=True)
                        pe.matmul(count_ps[:, 1, :], ones16[:, :], picked, start=True, stop=True)\
                            .then_inc(s["counts_done"], 1)
                    if f == 4 and not is_last(G):
                        if next_kind(G, routed) == "routed":
                            pe.wait_ge(s["xrow_loaded"], 16 * (G + (2 - NSH)))
                            transpose_rows(routed_source)
                        else:
                            transpose_rows(shared_source(G + 1))
                if is_last(G):
                    for f in range(FC - 2, FC):
                        down(G, parity, e, f)

            pe.wait_ge(s["xf_ready"], B)
            pe.wait_ge(s["pads_stored"], PAD_STEPS * 16)
            pe.wait_ge(s["ident_set"], 2)
            pe.wait_ge(s["ident16_set"], 1)
            pe.wait_ge(s["ones_set"], 1)
            pe.wait_ge(s["k2_ready"], B)
            pe.wait_ge(s["v2_ready"], B)
            pe.wait_ge(s["pT_copied"], B)
            transpose_rows(shared_source(0))
            pe.wait_ge(s["x2_ready"], B)
            pe.wait_ge(s["logits_copied"], B)
            stream(pe, body)


_INS = ['x', 'ctx_1024', 'L0_attn_W', 'L0_xattn_Wq', 'L0_xattn_bq', 'L0_xattn_Wk', 'L0_xattn_bk', 'L0_xattn_Wv',
        'L0_xattn_bv', 'L0_ffn_Wfc_s', 'L0_ffn_bfc_s', 'L0_ffn_Wproj_s', 'L0_ffn_bproj_s', 'L0_ffn_Wr',
        'L0_ffn_Wfc', 'L0_ffn_bfc', 'L0_ffn_Wproj', 'L0_ffn_bproj']


def kernel(**inputs):
    import numpy as np
    import concourse.bacc as bacc
    from concourse.bass_utils import run_bass_kernel_spmd

    nc = bacc.Bacc("TRN2", target_bir_lowering=False, num_devices=1)
    arrays, args = {}, []
    for name in _INS:
        a = np.ascontiguousarray(inputs[name])
        arrays["in_" + name] = a
        args.append(nc.dram_tensor("in_" + name, a.shape, mybir.dt.from_np(a.dtype), kind="ExternalInput").ap())
    out = nc.dram_tensor("out", inputs["x"].shape, F32, kind="ExternalOutput").ap()
    decoder_layer(nc, *args, out)
    r = run_bass_kernel_spmd(nc, [arrays], core_ids=[0])
    return r.results[0]["out"]
```

```python
from contextlib import ExitStack

import concourse.bass as bass
from concourse import mybir

F32 = mybir.dt.float32
F16 = mybir.dt.float16
I32 = mybir.dt.int32
U32 = mybir.dt.uint32
ALU = mybir.AluOpType
ACT = mybir.ActivationFunctionType
AX = mybir.AxisListType
ds = bass.ds

P = 128
LN_EPS = 1e-5
ATTN_EPS = 1e-6
W_SCALE = 256.0
A_SCALE = 16.0
UNSCALE = 1.0 / (W_SCALE * A_SCALE)
LAG = 4


def decoder_layer(nc, x, ctx_in, attn_w, wq_in, bq_in, wk_in, bk_in, wv_in, bv_in,
                  fc_s, bfc_s, proj_s, bproj_s, wr_in, fc, bfc, proj, bproj, out):
    B, S, D = x.shape
    CK = ctx_in.shape[1]
    E, _, H = fc.shape
    T = B * S
    TB = S // P
    TILES = T // P
    DK = D // P
    FC = H // P
    BLK = S
    NSH = T // BLK
    NRT = 2 * T // BLK + E - 1
    NBLK = NSH + NRT
    ROW = D + E + 1
    HALVES = 2 * (E + 1)
    SCALE = float(D) ** -0.5
    PADS = 3
    PAD_STEPS = NRT // PADS
    assert NRT % 4 == 3 and NRT % PADS == 0 and PAD_STEPS == B - 3
    assert S == 256 and D == 256 and H == 1024 and CK <= P

    rows_dram = nc.dram_tensor("rows_by_expert", [NRT * BLK, ROW], F32).ap()
    x2_dram = nc.dram_tensor("x2_residual", [T, D], F32).ap()

    def tiles_of(ap, b):
        return ap.rearrange("(b t p) n -> b p t n", t=TB, p=P)[ds(b, 1)].rearrange("b p t n -> p (b t) n")

    out_rows = out.rearrange("b s d -> (b s) d")
    x_rows = x.rearrange("b s d -> (b s) d")

    with ExitStack() as stack:
        def sb(name, shape, dt):
            return stack.enter_context(nc.sbuf_tensor(name, shape, dt))

        def pb(name, shape, dt=F32):
            return stack.enter_context(nc.psum_tensor(name, shape, dt))

        def sem(name):
            return stack.enter_context(nc.semaphore(name))

        w1 = sb("w1_parts", [P, HALVES * 2048], F16)
        w2 = sb("w2_parts", [P, HALVES * 2048], F16)
        rows = sb("rows", [P, TILES, ROW], F32)
        rows16 = rows[:, :, :].bitcast(F16)
        rows_i = rows[:, :, :].bitcast(I32)
        stage1 = sb("stage_w1", [P, 1024], F32)
        stage2 = sb("stage_w2", [P, 4, 256], F32)
        ident = sb("ident", [P, P], F32)
        ident16 = sb("ident16", [P, P], F16)
        earlier = sb("earlier", [P, P], F16)
        ones16 = sb("ones16", [P, P], F16)
        NB1 = (E + 1) * FC
        bias_cols = sb("bias_columns", [P, NB1 + 2 * DK], F32)
        bq = bias_cols[:, NB1:NB1 + DK]
        bk = bias_cols[:, NB1 + DK:NB1 + 2 * DK]
        stats = sb("stats", [P, 3, TB, 6], F32)
        mv = sb("mean_var", [P, 3, TB, 2], F32)
        var_eps = sb("var_eps", [P, 3 * TB], F32)
        minus_half = sb("minus_half", [P, 3 * TB], F32)
        carrier = sb("wait_carrier", [P, 1], F32)
        rstd = sb("rstd", [P, 3 * TB], F32)
        nmax = sb("nmax", [P, TB], F32)
        nbias = sb("nbias", [P, TB], F32)
        psum_p = sb("p_sum", [P, TB], F32)
        rinv = sb("rinv", [P, TB], F32)
        zden = sb("z_den", [P, TB], F32)
        zinv = sb("z_inv", [P, TB], F32)
        lg = sb("logits", [P, TB, E], F32)
        max8 = sb("max8", [P, TB, 8], F32)
        max8_at = sb("max8_at", [P, TB, 8], U32)
        top = sb("top_values", [P, TILES, 2], F32)
        top_f = sb("top_experts", [P, TILES, 2], F32)
        dest = sb("dest_rows", [P, 2, TILES], I32)
        blk_expert = sb("block_expert", [P, NRT], I32)

        FW = ROW * TB + 512 + 1024 + 512 + 1024 + 512 + 256
        fbuf = sb("expert_buffers", [P, FW], F32)
        at = [0]

        def cut(n):
            at[0] += n
            return fbuf[:, at[0] - n:at[0]]

        xrow = cut(ROW * TB).rearrange("p (t w) -> p t w", t=TB)
        x2blk = cut(512).rearrange("p (t n) -> p t n", t=TB)
        xT = [cut(512).bitcast(F16).rearrange("p (k l n) -> p k l n", k=DK, l=2) for _ in range(2)]
        g32 = [cut(256) for _ in range(2)]
        gs = [cut(256).bitcast(F16).rearrange("p (l n) -> p l n", l=2) for _ in range(4)]
        ybuf = cut(512).rearrange("p (t n) -> p t n", t=TB)
        b2blk = cut(256)
        gate = [sb(f"gate{i}", [P, TB], F32) for i in range(2)]
        token = [sb(f"token{i}", [P, TB], I32) for i in range(2)]

        last = (HALVES - 6) * 2048
        tail1 = w1[:, last:last + 4 * 2048].bitcast(F32)
        tail2 = w2[:, last:last + 4 * 2048].bitcast(F32)
        regions = [[tail1, 0, 4096], [tail2, 0, 4096], [fbuf, 0, FW]]

        def lend(n, pattern=None, **dims):
            for r in regions:
                if r[2] - r[1] >= n:
                    r[1] += n
                    ap = r[0][:, r[1] - n:r[1]]
                    return ap.rearrange(pattern, **dims) if pattern else ap
            raise ValueError("no room")

        proj16 = lend(DK * 4 * D).bitcast(F16).rearrange("p (k l n) -> p k l n", k=DK, l=2)
        wk = lend(DK * D, "p (k n) -> p k n", k=DK)
        wv = lend(DK * D, "p (k n) -> p k n", k=DK)
        xn = [lend(TB * D, "p (t n) -> p t n", t=TB) for _ in range(3)]
        xnT = [lend(DK * S).bitcast(F16).rearrange("p (k l n) -> p k l n", k=DK, l=2) for _ in range(2)]
        xnT.append(lend(DK * S, "p (k n) -> p k n", k=DK))
        expk = lend(TB * D, "p (t n) -> p t n", t=TB)
        expq = lend(DK * S, "p (k n) -> p k n", k=DK)
        kfeat = lend(TB * D, "p (t n) -> p t n", t=TB)
        qfeatT = lend(DK * S, "p (k n) -> p k n", k=DK)
        q2T = lend(DK * S, "p (k n) -> p k n", k=DK)
        vones = lend(TB * (D + 1), "p (t n) -> p t n", t=TB)
        state = lend(DK * (D + 1), "p (k n) -> p k n", k=DK)
        ctx_sb = lend(D)
        ctxT = lend(DK * CK, "p (k n) -> p k n", k=DK)
        k2T = lend(DK * CK, "p (k n) -> p k n", k=DK)
        v2 = lend(D)
        bv = lend(D)
        prob = lend(TB * CK, "p (t n) -> p t n", t=TB)
        probT = lend(S)
        wr = lend(DK * E, "p (k n) -> p k n", k=DK)
        pad_row = lend(ROW)
        bias_rows = lend(P)

        flat_stage = [stage1[:, :], stage2[:, :, :].rearrange("p c n -> p (c n)")]

        route = [[tail2, 0, 4096]]

        def scratch(n):
            route[0][1] += n
            return tail2[:, route[0][1] - n:route[0][1]]

        TE = TILES * E

        def te(ap):
            return ap.rearrange("p (t e) -> p t e", e=E)

        hot = [te(scratch(TE)) for _ in range(2)]
        gated = te(scratch(TE))
        picked = scratch(TE).bitcast(F16)[:, 0:TE]
        iota_te = te(scratch(TE))
        iota_i = scratch(TE).bitcast(I32)
        dlog = scratch(TILES)
        edlog = scratch(TILES)
        gden = scratch(TILES)
        g1 = scratch(TILES)
        g2 = scratch(TILES)
        totals = scratch(TE).rearrange("p (e t) -> p e t", e=E)
        keep = scratch(TE).rearrange("p (e t) -> p e t", e=E)
        upto = scratch(TE).rearrange("p (e t) -> p e t", e=E)
        base = scratch(TE).rearrange("p (e t) -> p e t", e=E)
        place = te(scratch(TE))
        chosen = te(scratch(TE))
        dest_f = scratch(2 * TILES).rearrange("p (j t) -> p j t", j=2)
        nblk_i = scratch(E).bitcast(I32)
        nblk_i2 = scratch(E).bitcast(I32)
        nblk = scratch(E)
        ones_e = scratch(E)
        blk_end = scratch(E)
        first_row = scratch(E)
        past = scratch(NRT * E).rearrange("p (n e) -> p n e", e=E)
        iota_blk = scratch(NRT)
        iota_blk_i = scratch(NRT).bitcast(I32)
        blk_f = scratch(NRT)

        bank0 = pb("bank0", [P, 512])
        bank_kv = pb("bank_kv", [P, 2, 512])
        bank3 = pb("bank3", [P, 512])
        bank_st = pb("bank_st", [P, 2, 512])
        bank6 = pb("bank6", [P, 512])
        bank7 = pb("bank7", [P, 512])

        tr = bank0[:, :].rearrange("p (k n) -> p k n", k=DK)
        qps = bank3[:, :].rearrange("p (k n) -> p k n", k=DK)
        q2ps = bank6[:, :].rearrange("p (k n) -> p k n", k=DK)
        ctxT_ps = bank7[:, 0:DK * CK].rearrange("p (k n) -> p k n", k=DK)
        k2T_ps = bank7[:, 256:256 + DK * CK].rearrange("p (k n) -> p k n", k=DK)
        v2_ps = bank7[:, 0:D]
        sc_ps = bank7[:, 0:TB * CK].rearrange("p (t n) -> p t n", t=TB)
        pT_ps = bank7[:, 0:S]
        pv_ps = bank_kv[:, 0, :].rearrange("p (t n) -> p t n", t=TB)
        lg_ps = bank_kv[:, 1, 0:TB * E].rearrange("p (t n) -> p t n", t=TB)
        count_ps = bank6[:, :].rearrange("p (j n) -> p j n", j=2)
        hid = [bank0, bank3]
        ypair = [bank_kv, bank_st]
        rowT_ps = bank7[:, :].bitcast(F16)

        s = {}
        for name in ("proj_loaded proj_hi proj_lo const_loaded x_loaded ctx_loaded w1_loaded w2_loaded x2_stored pads_stored "
                     "ident16_set ones_set ident_set pow_set biasT_done bias_ready "
                     "sums_step stats_step var_ready rstd_ready xn1_ready xn2_ready xn3_ready "
                     "t1_done t2_done t3_done t1_copied t2_copied t1_split t2_split t3_copied "
                     "kv_done q_done expk_ready v_copied expq_ready reluk_ready reluq_ready kfeat_ready qfeat_ready "
                     "state_done state_copied attn_done z_step x1_ready "
                     "ctxT_done ctxT_copied k2v2_done k2_ready v2_ready q2_done q2_ready "
                     "scores_done smax_step smax_ready p_ready rinv_ready pT_done pT_copied pv_done x2_ready "
                     "logits_done logits_copied max_step top_step top_ready hi_step xf_ready w1_hi w2_hi w1_lo w2_lo "
                     "route_step route_iota last_w1_loaded last_w2_loaded last_hi last_lo exp_gate counts_done picked_ready routed rows_sent "
                     "up_done gelu_done g_hi g_ready down_done y_read y_ready rowT_done xT_ready "
                     "meta_taken carried xrow_loaded x2blk_loaded b2_loaded y_stored y_added").split():
            s[name] = sem(name)

        block = stack.enter_context(nc.Block())

        def live(b):
            return not isinstance(b, int) or 0 <= b < B

        def got(eng, name, b):
            eng.wait_ge(s[name], b + 1)

        def got_if(eng, name, b):
            if isinstance(b, int):
                b = min(b, B - 1)
                if b < 0:
                    return
            eng.wait_ge(s[name], b + 1)

        def apart(eng):
            eng.wait_ge(s["ones_set"], 1)

        def steps(eng, step, first, end):
            for i in range(-2, first):
                step(i)
            with eng.Fori(first, end) as i:
                step(i)
            for i in range(end, B + LAG + 1):
                step(i)

        def half_of(i):
            if isinstance(i, int) and not LAG <= i < B:
                return 2 * E + i if i in (0, 1) else None
            return i - LAG

        def part_count(i):
            if isinstance(i, int) and not LAG <= i < B:
                return min(max(i, 0), 2)
            return i - (LAG - 2)

        def stream(eng, body):
            body(0, 0, False, None)
            body(1, 1, False, "shared")
            with eng.Fori(1, NSH // 2 - 1) as j:
                for c in range(2):
                    body(2 * j + c, c, False, "shared")
            body(NSH - 2, 0, False, "shared")
            body(NSH - 1, 1, False, "shared")
            body(NSH, 0, True, "shared")
            body(NSH + 1, 1, True, "routed")
            with eng.Fori(0, (NRT - 3) // 4) as j:
                for c in range(4):
                    body(4 * j + (NSH + 2 + c), c % 2, True, "routed", at_start=c == 0)
            body(NBLK - 1, 0, True, "routed", at_start=True)

        def is_last(G):
            return isinstance(G, int) and G == NBLK - 1

        def next_kind(G, routed):
            if is_last(G):
                return None
            return "routed" if routed or (isinstance(G, int) and G == NSH - 1) else "shared"

        w1_half = fc.rearrange("e (k p) f -> (e k) p f", p=P)
        w2_half = proj.rearrange("e (h c p) n -> (e h) p c n", p=P, c=4)

        @block.sync
        def _(sp):
            def load(dst, src):
                sp.dma_start(dst, src).then_inc(s["const_loaded"], 16)

            sp.dma_start(rows[:, 0:TB, 0:D], tiles_of(x_rows, 0)).then_inc(s["x_loaded"], 16)
            for k in range(DK):
                rows_k = slice(k * P, (k + 1) * P)
                sp.dma_start(flat_stage[k][:, 0:3 * D], attn_w[rows_k, :]).then_inc(s["proj_loaded"], 16)
                sp.dma_start(flat_stage[k][:, 3 * D:4 * D], wq_in[rows_k, :]).then_inc(s["proj_loaded"], 16)
            load(wk, wk_in.rearrange("(k p) n -> p k n", p=P))
            load(wv, wv_in.rearrange("(k p) n -> p k n", p=P))
            load(wr, wr_in.rearrange("(k p) n -> p k n", p=P))
            load(bias_rows[0:E * FC, :], bfc.rearrange("e (c p) -> (e c) p", p=P))
            load(bias_rows[E * FC:NB1, :], bfc_s.rearrange("(c p) -> c p", p=P))
            load(bias_rows[NB1:NB1 + DK, :], bq_in.rearrange("(k p) -> k p", p=P))
            load(bias_rows[NB1 + DK:NB1 + 2 * DK, :], bk_in.rearrange("(k p) -> k p", p=P))
            load(bv, bv_in.rearrange("(a n) -> a n", a=1).broadcast_to([P, D]))
            w1_shared = fc_s.rearrange("(k p) f -> k p f", p=P)
            w2_shared = proj_s.rearrange("(h c p) n -> h p c n", p=P, c=4)

            def load_half(half, before):
                shared = isinstance(half, int) and half >= 2 * E
                a = w1_shared[half - 2 * E] if shared else w1_half[ds(half, 1)].rearrange("a p f -> p (a f)")
                c = w2_shared[half - 2 * E] if shared else w2_half[ds(half, 1)].rearrange("a p c n -> p (a c) n")
                sp.wait_ge(s["w1_lo"], before)
                sp.dma_start(stage1[:, :], a).then_inc(s["w1_loaded"], 16)
                sp.wait_ge(s["w2_lo"], before)
                sp.dma_start(stage2[:, :, :], c).then_inc(s["w2_loaded"], 16)

            def step(i):
                if isinstance(i, int) and i == 0:
                    sp.wait_ge(s["proj_lo"], 1)
                if (half := half_of(i)) is not None:
                    load_half(half, part_count(i))
                if not isinstance(i, int) or 1 <= i <= PAD_STEPS:
                    n = i - 1
                    sp.dma_start(rows_dram.rearrange("(n q p) w -> n p q w", p=P, q=PADS * TB)[ds(n, 1)]
                                 .rearrange("n p q w -> p (n q) w"),
                                 pad_row.rearrange("p (q w) -> p q w", q=1).broadcast_to([P, PADS * TB, ROW]))\
                        .then_inc(s["pads_stored"], 16)
                b = i + 3
                if (isinstance(b, int) and 1 <= b < B) or not isinstance(b, int):
                    sp.wait_ge(s["x_loaded"], b * 16)
                    sp.dma_start(rows[:, ds(b * TB, TB), 0:D], tiles_of(x_rows, b)).then_inc(s["x_loaded"], 16)
                if live(i - 1):
                    b = i - 1
                    sp.wait_ge(s["ctxT_done"], b)
                    sp.dma_start(ctx_sb[0:CK, :], ctx_in[ds(b, 1)].rearrange("b s d -> s (b d)"))\
                        .then_inc(s["ctx_loaded"], 16)
                if live(i - 3):
                    b = i - 3
                    got(sp, "x2_ready", b)
                    sp.wait_ge(s["x2_stored"], b * 16)
                    sp.dma_start(tiles_of(x2_dram, b), rows[:, ds(b * TB, TB), 0:D])\
                        .then_inc(s["x2_stored"], 16)

            sp.wait_ge(s["pow_set"], 4)
            steps(sp, step, LAG, B - 3)

            sp.wait_ge(s["logits_done"], B)
            sp.wait_ge(s["pads_stored"], PAD_STEPS * 16)

            def load_b2(G, e):
                sp.wait_ge(s["y_read"], G)
                src = bproj_s.rearrange("(a n) -> a n", a=1) if isinstance(e, int) else bproj[ds(e, 1)]
                sp.dma_start(b2blk, src.broadcast_to([P, D])).then_inc(s["b2_loaded"], 16)

            def finish_shared(G):
                got(sp, "y_ready", G)
                sp.dma_start(tiles_of(out_rows, G), ybuf).then_inc(s["y_stored"], 16)

            def shared_block(G):
                if isinstance(G, int) and G == 0:
                    sp.wait_ge(s["x2_stored"], B * 16)
                else:
                    sp.wait_ge(s["y_ready"], G)
                sp.dma_start(x2blk, tiles_of(x2_dram, G)).then_inc(s["x2blk_loaded"], 16)
                load_b2(G, E)
                if not (isinstance(G, int) and G == 0):
                    finish_shared(G - 1)

            for G in range(3):
                shared_block(G)
            sp.wait_ge(s["routed"], 1)
            load_half(2 * E - 4, HALVES - 4)
            with sp.Fori(1, NSH // 2 - 1) as j:
                for c in range(2):
                    shared_block(2 * j + (1 + c))
            sp.wait_ge(s["rows_sent"], 2 * TILES * 16)

            def load_rows(n):
                sp.wait_ge(s["meta_taken"], n)
                sp.dma_start(xrow, tiles_of(rows_dram, n)).then_inc(s["xrow_loaded"], 16)

            def expert_of(n):
                return sp.value_load(blk_expert[0:1, ds(n, 1)], min_val=0, max_val=E - 1)

            load_rows(0)
            shared_block(NSH - 1)
            load_rows(1)
            load_b2(NSH, expert_of(0))
            finish_shared(NSH - 1)
            with sp.Fori(1, NRT - 1) as n:
                load_rows(n + 1)
                load_b2(n + NSH, expert_of(n))
            load_b2(NRT - 1 + NSH, expert_of(NRT - 1))

        @block.gpsimd
        def _(pool):
            pool.memset(minus_half[:, :], -0.5)
            pool.memset(pad_row, 0.0).then_inc(s["pow_set"], 1)
            pool.memset(ident[:, :], 0.0).then_inc(s["pow_set"], 1)
            pool.memset(earlier[:, :], 1.0).then_inc(s["pow_set"], 1)
            pool.wait_ge(s["pow_set"], 2)
            pool.affine_select(out=ident[:, :], in_=ident[:, :], compare_op=ALU.not_equal, fill=1.0,
                               base=0, pattern=[[-1, P]], channel_multiplier=1).then_inc(s["ident_set"], 1)
            pool.memset(pad_row.bitcast(I32)[:, ROW - 1:ROW], T).then_inc(s["pow_set"], 1)
            pool.wait_ge(s["pow_set"], 3)
            pool.affine_select(out=earlier[:, :], in_=earlier[:, :], compare_op=ALU.is_gt, fill=0.0,
                               base=0, pattern=[[1, P]], channel_multiplier=-1).then_inc(s["ident_set"], 1)
            pool.wait_ge(s["ident_set"], 1)
            pool.tensor_copy(ident16[:, :], ident[:, :]).then_inc(s["ident16_set"], 1)

            def convert_lo(half, before):
                pool.wait_ge(s["w1_hi"], before + 1)
                pool.tensor_tensor(w1[:, ds(half * 2048 + 1024, 1024)], stage1[:, :], w1[:, ds(half * 2048, 1024)],
                                   ALU.subtract).then_inc(s["w1_lo"], 1)

            def step(i):
                if (half := half_of(i)) is not None:
                    convert_lo(half, part_count(i))
                if not isinstance(i, int) or i < B + LAG - 1:
                    pool.wait_ge(s["var_ready"], i + 3)
                    pool.tensor_tensor(rstd[:, :], var_eps[:, :], minus_half[:, :], ALU.pow)\
                        .then_inc(s["rstd_ready"], 1)

            steps(pool, step, LAG, B)

            pool.wait_ge(s["logits_done"], B)
            pool.wait_ge(s["xf_ready"], B)
            pool.iota(iota_i, [[0, TILES], [1, E]], base=0, channel_multiplier=0).then_inc(s["route_iota"], 1)
            pool.iota(iota_blk_i, [[1, NRT]], base=0, channel_multiplier=0).then_inc(s["route_iota"], 1)
            pool.memset(keep, 1.0).then_inc(s["route_iota"], 1)
            pool.memset(ones_e, 1.0)
            pool.wait_ge(s["route_iota"], 3)
            pool.memset(keep[:, :, 0:1], 0.0).then_inc(s["route_iota"], 1)
            pool.iota(rows_i[:, :, ROW - 1], [[P, TILES]], base=0, channel_multiplier=1)\
                .then_inc(s["route_iota"], 1)

            pool.wait_ge(s["route_iota"], 5)
            pool.wait_ge(s["routed"], 1)
            pool.wait_ge(s["pads_stored"], PAD_STEPS * 16)
            for t in range(TILES):
                for j in range(2):
                    pool.indirect_dma_start(
                        out=rows_dram, out_offset=bass.IndirectOffsetOnAxis(ap=dest[:, j, t:t + 1].bitcast(U32), axis=0),
                        in_=rows[:, t, :], in_offset=None).then_inc(s["rows_sent"], 16)

            staged = ((w1, stage1[:, :], w1_half, stage1[:, :], "w1_loaded"),
                      (w2, flat_stage[1], w2_half, stage2[:, :, :], "w2_loaded"))
            for q in range(4):
                half = 2 * E - 4 + q
                for k, (w, stage, weights, dst, loaded) in enumerate(staged):
                    hi = w[:, half * 2048:half * 2048 + 1024]
                    lo = w[:, half * 2048 + 1024:half * 2048 + 2048]
                    if q == 0:
                        pool.wait_ge(s[loaded], (HALVES - 3) * 16)
                    else:
                        pool.wait_ge(s["last_" + loaded], q * 16)
                    pool.tensor_scalar(stage, stage, W_SCALE, None, ALU.mult).then_inc(s["last_hi"], 1)
                    pool.wait_ge(s["last_hi"], 4 * q + 2 * k + 1)
                    pool.tensor_copy(hi, stage).then_inc(s["last_hi"], 1)
                    pool.wait_ge(s["last_hi"], 4 * q + 2 * k + 2)
                    pool.tensor_tensor(lo, stage, hi, ALU.subtract).then_inc(s["last_lo"], 1)
                    if q < 3:
                        pool.wait_ge(s["last_lo"], 2 * q + k + 1)
                        pool.dma_start(dst, weights[half + 1]).then_inc(s["last_" + loaded], 16)

            last_token = pool.to_reg(T - 1)

            def add_block(n, parity):
                pool.wait_ge(s["y_ready"], n + (NSH + 1))
                pool.wait_ge(s["carried"], n)
                if isinstance(n, int) and n == 0:
                    pool.wait_ge(s["y_stored"], NSH * 16)
                else:
                    pool.wait_ge(s["y_added"], n * (16 * TB))
                pool.tensor_tensor(carrier[:, :], minus_half[:, 0:1], minus_half[:, 0:1], ALU.add)\
                    .then_inc(s["carried"], 1)
                for t in range(TB):
                    pool.indirect_dma_start(
                        out=out_rows, out_offset=bass.IndirectOffsetOnAxis(ap=token[parity][:, t:t + 1].bitcast(U32), axis=0),
                        in_=ybuf[:, t, :], in_offset=None, bounds_check=last_token, oob_is_err=False,
                        compute_op=ALU.add).then_inc(s["y_added"], 16)

            add_block(0, 0)
            with pool.Fori(0, (NRT - 1) // 2) as j:
                for c in range(2):
                    add_block(2 * j + (1 + c), (1 + c) % 2)
            pool.wait_ge(s["y_added"], NRT * TB * 16)

        @block.scalar
        def _(act):
            def copy(dst, src, name):
                act.activation(dst, src, ACT.Copy).then_inc(s[name], 1)

            def convert_w1(half, before):
                act.wait_ge(s["w1_loaded"], (before + 1) * 16)
                act.activation(w1[:, ds(half * 2048, 1024)], stage1[:, :], ACT.Copy, scale=W_SCALE)
                act.activation(stage1[:, :], stage1[:, :], ACT.Copy, scale=W_SCALE).then_inc(s["w1_hi"], 1)

            def convert_w2(half, before):
                act.wait_ge(s["w2_loaded"], (before + 1) * 16)
                act.activation(w2[:, ds(half * 2048, 1024)], flat_stage[1], ACT.Copy, scale=W_SCALE)\
                    .then_inc(s["w2_hi"], 1)

            def step(i):
                if live(i):
                    got(act, "t1_done", i)
                    act.activation(xnT[0][:, :, 0, :], tr, ACT.Copy, scale=A_SCALE).then_inc(s["t1_copied"], 1)
                if live(i - 1):
                    got(act, "state_done", i - 1)
                    copy(state, bank_st[:, :, 0:D + 1], "state_copied")
                if (half := half_of(i)) is not None:
                    convert_w1(half, part_count(i))
                if live(i - 3):
                    b = i - 3
                    got(act, "smax_ready", b)
                    got_if(act, "pT_done", b - 1)
                    for t in range(TB):
                        op = act.activation(prob[:, t, :], sc_ps[:, t, :], ACT.Exp, bias=nbias[:, t:t + 1],
                                            scale=SCALE, accum_out=psum_p[:, t:t + 1])
                    op.then_inc(s["p_ready"], 1)
                if (half := half_of(i)) is not None:
                    convert_w2(half, part_count(i))
                if live(i):
                    got(act, "kv_done", i)
                    got_if(act, "kfeat_ready", i - 1)
                    act.activation(expk, bank_kv[:, :, 0:D], ACT.Exp, scale=UNSCALE).then_inc(s["expk_ready"], 1)
                    got_if(act, "state_done", i - 1)
                    act.activation(kfeat, bank_kv[:, :, 0:D], ACT.Relu, scale=UNSCALE).then_inc(s["reluk_ready"], 1)
                    act.activation(vones[:, :, 0:D], bank_kv[:, :, D:2 * D], ACT.Copy, scale=UNSCALE)\
                        .then_inc(s["v_copied"], 1)
                    got(act, "q_done", i)
                    got_if(act, "qfeat_ready", i - 1)
                    act.activation(expq, qps, ACT.Exp, scale=UNSCALE).then_inc(s["expq_ready"], 1)
                if live(i - 3):
                    got(act, "pT_done", i - 3)
                    got_if(act, "pv_done", i - 4)
                    copy(probT[0:CK, :], pT_ps[0:CK, :], "pT_copied")
                if live(i - 2):
                    got(act, "t2_done", i - 2)
                    act.activation(xnT[1][:, :, 0, :], tr, ACT.Copy, scale=A_SCALE).then_inc(s["t2_copied"], 1)
                if live(i):
                    got_if(act, "attn_done", i - 1)
                    act.activation(qfeatT, qps, ACT.Relu, scale=UNSCALE).then_inc(s["reluq_ready"], 1)
                if live(i - 2):
                    got(act, "ctxT_done", i - 2)
                    copy(ctxT, ctxT_ps, "ctxT_copied")
                if isinstance(i, int) and i == B + LAG - 1:
                    got(act, "rowT_done", 0)
                    copy(xT[0].rearrange("p k l n -> p (k l n)"), rowT_ps, "xT_ready")
                if live(i - 4):
                    got(act, "t3_done", i - 4)
                    copy(xnT[2], tr, "t3_copied")
                if isinstance(i, int) and i == 0:
                    act.wait_ge(s["biasT_done"], 1)
                    copy(bias_cols[:, :], bank6[:, 0:NB1 + 2 * DK], "bias_ready")
                    act.wait_ge(s["bias_ready"], 1)
                if live(i - 2):
                    got(act, "k2v2_done", i - 2)
                    for m in range(DK):
                        op = act.activation(k2T[:, m, :], k2T_ps[:, m, :], ACT.Identity, bias=bk[:, m:m + 1])
                    op.then_inc(s["k2_ready"], 1)
                    got(act, "q2_done", i - 2)
                    for m in range(DK):
                        op = act.activation(q2T[:, m, :], q2ps[:, m, :], ACT.Identity, bias=bq[:, m:m + 1],
                                            scale=UNSCALE)
                    op.then_inc(s["q2_ready"], 1)

            act.wait_ge(s["proj_loaded"], 2 * DK * 16)
            for k in range(DK):
                op = act.activation(proj16[:, k, 0, :], flat_stage[k], ACT.Copy, scale=W_SCALE)
            op.then_inc(s["proj_hi"], 1)
            steps(act, step, LAG + 1, B)

            act.wait_ge(s["route_step"], 1)
            act.activation(edlog, dlog, ACT.Exp).then_inc(s["exp_gate"], 1)

            def body(G, parity, routed, before, at_start=False):
                e = E
                if routed:
                    e = act.value_load(blk_expert[0:1, ds(G - NSH, 1)], min_val=0, max_val=E - 1)
                for f in range(FC):
                    got(act, "up_done", FC * G + f)
                    if not (isinstance(G, int) and FC * G + f < 2):
                        act.wait_ge(s["g_ready"], FC * G + (f - 1))
                    bias = bias_cols[:, ds(e * FC + f, 1)]
                    act.activation(g32[f % 2], hid[f % 2][:, 0:BLK], ACT.Gelu_apprx_tanh, bias=bias,
                                   scale=UNSCALE).then_inc(s["gelu_done"], 1)
                    if f == 5 and not is_last(G):
                        got(act, "rowT_done", G + 1)
                        copy(xT[1 - parity].rearrange("p k l n -> p (k l n)"), rowT_ps, "xT_ready")

            act.wait_ge(s["logits_done"], B)
            stream(act, body)

        @block.vector
        def _(dve):
            route_count = [0]

            def chain(op, name, count, own=False):
                op.then_inc(s[name], 1)
                if own:
                    apart(dve)
                dve.wait_ge(s[name], count)

            def layer_norm(n, b):
                got_if(dve, f"t{n + 1}_done", b - 1)
                if n == 2:
                    got_if(dve, "xf_ready", b - 1)
                for t in range(TB):
                    r = rows[:, ds(b * TB + t, 1), 0:D].rearrange("p a n -> p (a n)")
                    op = dve.tensor_scalar(xn[n][:, t, :], r, mv[:, n, t, 0:1],
                                           rstd[:, n * TB + t:n * TB + t + 1], ALU.subtract, ALU.mult)
                op.then_inc(s[f"xn{n + 1}_ready"], 1)

            def split_lo(n):
                dve.scalar_tensor_tensor(xnT[n][:, :, 1, :], tr, A_SCALE, xnT[n][:, :, 0, :], ALU.mult, ALU.subtract)\
                    .then_inc(s[f"t{n + 1}_split"], 1)

            def step(i):
                if live(i - 5):
                    got(dve, "logits_done", i - 5)
                    dve.tensor_copy(lg[:, :, :], lg_ps).then_inc(s["logits_copied"], 1)
                if live(i):
                    got(dve, "t1_copied", i)
                    split_lo(0)
                if live(i + 1) or live(i - 2) or live(i - 4):
                    dve.wait_ge(s["rstd_ready"], i + 2)
                for n, b in ((1, i - 2), (2, i - 4), (0, i + 1)):
                    if live(b):
                        layer_norm(n, b)
                if isinstance(i, int) and i == -1:
                    dve.wait_ge(s["proj_hi"], 1)
                    for k in range(DK):
                        op = dve.scalar_tensor_tensor(proj16[:, k, 1, :], flat_stage[k], W_SCALE, proj16[:, k, 0, :],
                                                      ALU.mult, ALU.subtract)
                    op.then_inc(s["proj_lo"], 1)
                if live(i - 3):
                    b = i - 3
                    got(dve, "scores_done", b)
                    got_if(dve, "p_ready", b - 1)
                    chain(dve.reduce_max(nmax[:, :], sc_ps, AX.X, negate=True), "smax_step", b + 1)
                    dve.tensor_scalar(nbias[:, :], nmax[:, :], SCALE, None, ALU.mult).then_inc(s["smax_ready"], 1)
                if live(i - 4):
                    b = i - 4
                    dve.wait_ge(s["x2_stored"], (b + 1) * 16)
                    got(dve, "xn3_ready", b)
                    hi = rows16[:, ds(b * TB, TB), 0:D]
                    lo = rows16[:, ds(b * TB, TB), D:2 * D]
                    chain(dve.tensor_scalar(hi, xn[2], A_SCALE, None, ALU.mult), "hi_step", b + 1)
                    dve.scalar_tensor_tensor(lo, xn[2], A_SCALE, hi, ALU.mult, ALU.subtract).then_inc(s["xf_ready"], 1)
                if live(i - 5):
                    b = i - 5
                    apart(dve)
                    got(dve, "logits_copied", b)
                    for t in range(TB):
                        op = dve.max(max8[:, t, :], lg[:, t, :])
                    chain(op, "max_step", b + 1, own=True)
                    for t in range(TB):
                        op = dve.max_index(max8_at[:, t, :], max8[:, t, :], lg[:, t, :])
                    chain(op, "top_step", b + 1)
                    dve.tensor_copy(top[:, ds(b * TB, TB), :], max8[:, :, 0:2])
                    dve.tensor_copy(top_f[:, ds(b * TB, TB), :], max8_at[:, :, 0:2]).then_inc(s["top_ready"], 1)
                if (half := half_of(i)) is not None:
                    dve.wait_ge(s["w2_hi"], part_count(i) + 1)
                    dve.scalar_tensor_tensor(w2[:, ds(half * 2048 + 1024, 1024)], flat_stage[1], W_SCALE,
                                             w2[:, ds(half * 2048, 1024)], ALU.mult, ALU.subtract)\
                        .then_inc(s["w2_lo"], 1)
                if live(i):
                    got(dve, "reluk_ready", i)
                    dve.scalar_tensor_tensor(kfeat, expk, 1.0, kfeat, ALU.min, ALU.add).then_inc(s["kfeat_ready"], 1)
                if live(i - 2):
                    got(dve, "t2_copied", i - 2)
                    split_lo(1)
                if live(i - 3):
                    got(dve, "p_ready", i - 3)
                    dve.reciprocal(rinv[:, :], psum_p[:, :]).then_inc(s["rinv_ready"], 1)
                if live(i - 1):
                    b = i - 1
                    got(dve, "attn_done", b)
                    chain(dve.tensor_scalar(zden[:, :], bank_st[:, :, D], ATTN_EPS, None, ALU.add),
                          "z_step", 2 * b + 1)
                    chain(dve.reciprocal(zinv[:, :], zden[:, :]), "z_step", 2 * b + 2)
                    for t in range(TB):
                        r = rows[:, ds(b * TB + t, 1), 0:D].rearrange("p a n -> p (a n)")
                        op = dve.scalar_tensor_tensor(r, bank_st[:, t, 0:D], zinv[:, t:t + 1], r, ALU.mult, ALU.add)
                    op.then_inc(s["x1_ready"], 1)
                if live(i):
                    got(dve, "reluq_ready", i)
                    dve.scalar_tensor_tensor(qfeatT, expq, 1.0, qfeatT, ALU.min, ALU.add).then_inc(s["qfeat_ready"], 1)
                if live(i - 3):
                    b = i - 3
                    got(dve, "rinv_ready", b)
                    got(dve, "pv_done", b)
                    for t in range(TB):
                        r = rows[:, ds(b * TB + t, 1), 0:D].rearrange("p a n -> p (a n)")
                        op = dve.scalar_tensor_tensor(r, pv_ps[:, t, :], rinv[:, t:t + 1], r, ALU.mult, ALU.add)
                    op.then_inc(s["x2_ready"], 1)

                norms = [(n, b) for n, b in ((0, i + 2), (1, i - 1), (2, i - 3)) if live(b)]
                if norms:
                    for n, b in norms:
                        apart(dve)
                        if n == 0:
                            dve.wait_ge(s["x_loaded"], (b + 1) * 16)
                        else:
                            got(dve, "x1_ready" if n == 1 else "x2_ready", b)
                        for t in range(TB):
                            r = rows[:, ds(b * TB + t, 1), 0:D].rearrange("p a n -> p (a n)")
                            op = dve.bn_stats(stats[:, n, t, :], r)
                    chain(op, "sums_step", i + 3, own=True)
                    for n, b in norms:
                        for t in range(TB):
                            op = dve.bn_aggr(mv[:, n, t, :], stats[:, n, t, :])
                    chain(op, "stats_step", i + 3)
                    dve.tensor_scalar(var_eps[:, :].rearrange("p (n t) -> p n t", n=3), mv[:, :, :, 1], LN_EPS, None,
                                      ALU.add).then_inc(s["var_ready"], 1)
                if live(i - 2):
                    b = i - 2
                    got(dve, "k2_ready", b)
                    dve.tensor_tensor(v2[0:CK, :], v2_ps[0:CK, :], bv[0:CK, :], ALU.add).then_inc(s["v2_ready"], 1)

            dve.memset(mv[:, :, :, :], 1.0)
            dve.memset(vones[:, :, D:D + 1], 1.0)
            dve.memset(ones16[:, :], 1.0).then_inc(s["ones_set"], 1)
            dve.wait_ge(s["ones_set"], 1)
            steps(dve, step, LAG + 2, B - 2)

            def then(op):
                route_count[0] += 1
                chain(op, "route_step", route_count[0])

            def over_e(ap):
                return ap.rearrange("p (t a) -> p t a", a=1).broadcast_to([P, TILES, E])

            dve.wait_ge(s["top_ready"], B)
            then(dve.tensor_tensor(dlog, top[:, :, 1], top[:, :, 0], ALU.subtract))
            dve.wait_ge(s["route_iota"], 4)
            dve.tensor_copy(iota_te.rearrange("p t e -> p (t e)"), iota_i)
            then(dve.tensor_copy(iota_blk, iota_blk_i))
            for j in range(2):
                op = dve.tensor_tensor(hot[j], iota_te, top_f[:, :, j:j + 1].broadcast_to([P, TILES, E]), ALU.is_equal)
            then(op)
            dve.tensor_tensor(picked.rearrange("p (t e) -> p t e", e=E), hot[0], hot[1], ALU.add)\
                .then_inc(s["picked_ready"], 1)
            def route(part):
                if part == 0:
                    dve.wait_ge(s["exp_gate"], 1)
                    then(dve.tensor_scalar(gden, edlog, 1.0, None, ALU.add))
                    then(dve.reciprocal(g1, gden))
                elif part == 1:
                    then(dve.tensor_tensor(g2, g1, edlog, ALU.mult))
                    dve.tensor_tensor(gated, hot[0], over_e(g1), ALU.mult)
                elif part == 2:
                    then(dve.tensor_tensor(chosen, hot[1], over_e(g2), ALU.mult))
                    then(dve.tensor_tensor(rows[:, :, D:D + E], gated, chosen, ALU.add))
                elif part == 3:
                    dve.wait_ge(s["counts_done"], 1)
                    then(dve.tensor_copy(totals, count_ps[:, 1, :].rearrange("p (t e) -> p e t", e=E)))
                elif part == 4:
                    then(dve.tensor_tensor_scan(upto.rearrange("p e t -> p (e t)"), keep.rearrange("p e t -> p (e t)"),
                                                totals.rearrange("p e t -> p (e t)"), 0.0, ALU.mult, ALU.add))
                elif part == 5:
                    then(dve.tensor_scalar(nblk_i, upto[:, :, TILES - 1], float(BLK - 1), None, ALU.add))
                    then(dve.tensor_scalar(nblk_i2, nblk_i, BLK.bit_length() - 1, None, ALU.logical_shift_right))
                    then(dve.tensor_copy(nblk, nblk_i2))
                elif part == 6:
                    then(dve.tensor_tensor_scan(blk_end, ones_e, nblk, 0.0, ALU.mult, ALU.add))
                    then(dve.tensor_tensor(first_row, blk_end, nblk, ALU.subtract))
                elif part == 7:
                    dve.tensor_tensor(base, upto, totals, ALU.subtract)
                elif part == 8:
                    then(dve.tensor_tensor(past, iota_blk.rearrange("p (n a) -> p n a", a=1).broadcast_to([P, NRT, E]),
                                           blk_end.rearrange("p (a e) -> p a e", a=1).broadcast_to([P, NRT, E]),
                                           ALU.is_ge))
                elif part == 9:
                    then(dve.tensor_reduce(blk_f, past, AX.X, ALU.add))
                    dve.tensor_scalar(blk_expert[:, :], blk_f, float(E - 1), None, ALU.min)
                elif part == 10:
                    then(dve.scalar_tensor_tensor(
                        base, first_row.rearrange("p (e a) -> p e a", a=1).broadcast_to([P, E, TILES]), float(BLK),
                        base, ALU.mult, ALU.add))
                elif part == 11:
                    then(dve.tensor_tensor(place, te(count_ps[:, 0, :]), base.rearrange("p e t -> p t e"), ALU.add))
                elif part < 16:
                    j = (part - 12) // 2
                    if part % 2 == 0:
                        then(dve.tensor_tensor(chosen, place, hot[j], ALU.mult))
                    else:
                        then(dve.tensor_reduce(dest_f[:, j, :], chosen, AX.X, ALU.add))
                    if part == 15:
                        dve.tensor_copy(dest[:, :, :], dest_f).then_inc(s["routed"], 1)

            def evacuate(G, parity, shared):
                dve.wait_ge(s["down_done"], FC * (G + 1))
                dve.wait_ge(s["b2_loaded"], 16 * (G + 1))
                if not (isinstance(G, int) and G == 0):
                    if shared or (isinstance(G, int) and G == NSH):
                        dve.wait_ge(s["y_stored"], 16 * G)
                    else:
                        dve.wait_ge(s["y_added"], (16 * TB) * (G - NSH))
                for t in range(TB):
                    op = dve.scalar_tensor_tensor(ybuf[:, t, :], ypair[parity][:, t, 0:D], UNSCALE, b2blk,
                                                  ALU.mult, ALU.add)
                op.then_inc(s["y_read"], 1)
                dve.wait_ge(s["y_read"], G + 1)
                if shared:
                    dve.wait_ge(s["x2blk_loaded"], 16 * (G + 1))
                    dve.tensor_tensor(ybuf, ybuf, x2blk, ALU.add).then_inc(s["y_ready"], 1)
                else:
                    for t in range(TB):
                        op = dve.tensor_scalar(ybuf[:, t, :], ybuf[:, t, :], gate[parity][:, t:t + 1], None, ALU.mult)
                    op.then_inc(s["y_ready"], 1)

            def body(G, parity, routed, before, at_start=False):
                for f in range(FC):
                    c = FC * G + f
                    got(dve, "gelu_done", c)
                    if not (isinstance(c, int) and c < 4):
                        dve.wait_ge(s["down_done"], c - 3)
                    g = gs[f % 4]
                    chain(dve.tensor_scalar(g[:, 0, :], g32[f % 2], A_SCALE, None, ALU.mult), "g_hi", c + 1)
                    dve.scalar_tensor_tensor(g[:, 1, :], g32[f % 2], A_SCALE, g[:, 0, :], ALU.mult, ALU.subtract)\
                        .then_inc(s["g_ready"], 1)
                    if isinstance(G, int) and G < 2:
                        route(FC * G + f)
                    if f == 2 and not (isinstance(G, int) and G == 0):
                        evacuate(G - 1, 1 - parity, shared=before == "shared")
                    if f == 6 and next_kind(G, routed) == "routed":
                        n = G + (1 - NSH)
                        expert = dve.value_load(blk_expert[0:1, ds(n, 1)], min_val=0, max_val=E - 1)
                        got(dve, "rowT_done", G + 1)
                        if not (isinstance(n, int) and n < 2):
                            dve.wait_ge(s["y_added"], (n - 1) * (16 * TB))
                        dve.tensor_copy(gate[1 - parity][:, :],
                                        xrow[:, :, ds(expert + D, 1)].rearrange("p t a -> p (t a)"))
                        dve.tensor_copy(token[1 - parity][:, :], xrow[:, :, ROW - 1].bitcast(I32))\
                            .then_inc(s["meta_taken"], 1)

            dve.wait_ge(s["xf_ready"], B)
            stream(dve, body)
            evacuate(NBLK - 1, 0, shared=False)

        @block.tensor
        def _(pe):
            def tile(t):
                return slice(t * P, (t + 1) * P)

            def transpose_norm(n):
                for t in range(TB):
                    for k in range(DK):
                        op = pe.transpose(tr[:, k, tile(t)], xn[n][:, t, tile(k)], ident[:, :])
                return op

            PASSES = ((0, 0), (0, 1), (1, 0))

            def project_q(dst, first, x):
                for m in range(DK):
                    for k in range(DK):
                        for a, c in PASSES:
                            op = pe.matmul(dst[:, m, :], proj16[:, k, c, first + m * P:first + (m + 1) * P],
                                           x[:, k, a, :], start=(k, a, c) == (0, 0, 0), stop=(k, a, c) == (DK - 1, 1, 0))
                return op

            def transpose_rows(source):
                for k in range(DK):
                    for part in range(2):
                        for t in range(TB):
                            at = ((k * 2 + part) * TB + t) * P
                            op = pe.transpose(rowT_ps[:, at:at + P], source(t, part, k), ident16[:, :])
                op.then_inc(s["rowT_done"], 1)

            def shared_source(G):
                def source(t, part, k):
                    at = part * D + k * P
                    return rows16[:, ds(G * TB + t, 1), at:at + P].rearrange("p a n -> p (a n)")
                return source

            def step(i):
                if live(i):
                    got(pe, "xn1_ready", i)
                    got_if(pe, "t3_copied", i - 5)
                    transpose_norm(0).then_inc(s["t1_done"], 1)
                if live(i - 1):
                    b = i - 1
                    got(pe, "kfeat_ready", b)
                    got(pe, "v_copied", b)
                    got_if(pe, "x1_ready", b - 1)
                    for m in range(DK):
                        for t in range(TB):
                            op = pe.matmul(bank_st[:, m, 0:D + 1], kfeat[:, t, tile(m)], vones[:, t, :],
                                           start=t == 0, stop=t == TB - 1)
                    op.then_inc(s["state_done"], 1)
                if live(i - 3):
                    b = i - 3
                    got(pe, "q2_ready", b)
                    got(pe, "v2_ready", b)
                    for t in range(TB):
                        for m in range(DK):
                            op = pe.matmul(sc_ps[:, t, :], q2T[:, m, tile(t)], k2T[:, m, :], start=m == 0, stop=m == DK - 1)
                    op.then_inc(s["scores_done"], 1)
                if live(i):
                    if isinstance(i, int) and i == 0:
                        pe.wait_ge(s["proj_lo"], 1)
                    got(pe, "t1_split", i)
                    got_if(pe, "x2_ready", i - 4)
                    got_if(pe, "logits_copied", i - 5)
                    for t in range(TB):
                        for k in range(DK):
                            for a, c in PASSES:
                                op = pe.matmul(bank_kv[:, t, :], xnT[0][:, k, a, tile(t)], proj16[:, k, c, D:3 * D],
                                               start=(k, a, c) == (0, 0, 0), stop=(k, a, c) == (DK - 1, 1, 0))
                    op.then_inc(s["kv_done"], 1)
                    got_if(pe, "reluq_ready", i - 1)
                    op = project_q(qps, 0, xnT[0])
                    op.then_inc(s["q_done"], 1)
                if isinstance(i, int) and i == 0:
                    pe.wait_ge(s["const_loaded"], 8 * 16)
                    n = NB1 + 2 * DK
                    pe.transpose(bank6[:, 0:n], bias_rows[0:n, :], ident[0:n, 0:n]).then_inc(s["biasT_done"], 1)
                if live(i - 3):
                    got(pe, "p_ready", i - 3)
                    for t in range(TB):
                        op = pe.transpose(pT_ps[0:CK, tile(t)], prob[:, t, :], ident[:, :])
                    op.then_inc(s["pT_done"], 1)
                if live(i - 2):
                    got(pe, "xn2_ready", i - 2)
                    got_if(pe, "t1_split", i)
                    transpose_norm(1).then_inc(s["t2_done"], 1)
                if live(i - 1):
                    b = i - 1
                    got(pe, "state_copied", b)
                    got(pe, "qfeat_ready", b)
                    for t in range(TB):
                        for m in range(DK):
                            op = pe.matmul(bank_st[:, t, 0:D + 1], qfeatT[:, m, tile(t)], state[:, m, :],
                                           start=m == 0, stop=m == DK - 1)
                    op.then_inc(s["attn_done"], 1)
                if live(i - 2):
                    b = i - 2
                    pe.wait_ge(s["ctx_loaded"], (b + 1) * 16)
                    got_if(pe, "pT_copied", b - 1)
                    for k in range(DK):
                        op = pe.transpose(ctxT_ps[:, k, :], ctx_sb[0:CK, tile(k)], ident[0:CK, 0:CK])
                    op.then_inc(s["ctxT_done"], 1)
                if live(i - 3):
                    b = i - 3
                    got(pe, "pT_copied", b)
                    got_if(pe, "v_copied", i)
                    for t in range(TB):
                        op = pe.matmul(pv_ps[:, t, :], probT[0:CK, tile(t)], v2[0:CK, :], start=True, stop=True)
                    op.then_inc(s["pv_done"], 1)
                if isinstance(i, int) and i == B + LAG - 1:
                    pe.wait_ge(s["ident16_set"], 1)
                    got(pe, "k2_ready", B - 1)
                    got(pe, "v2_ready", B - 1)
                    got(pe, "pT_copied", B - 1)
                    got(pe, "xf_ready", 0)
                    transpose_rows(shared_source(0))
                if live(i - 4):
                    got(pe, "xn3_ready", i - 4)
                    got_if(pe, "t2_split", i - 2)
                    transpose_norm(2).then_inc(s["t3_done"], 1)
                if live(i - 2):
                    b = i - 2
                    got(pe, "ctxT_copied", b)
                    for m in range(DK):
                        for k in range(DK):
                            pe.matmul(k2T_ps[:, m, :], wk[:, k, tile(m)], ctxT[:, k, :], start=k == 0, stop=k == DK - 1)
                    for k in range(DK):
                        op = pe.matmul(v2_ps[0:CK, :], ctxT[:, k, :], wv[:, k, :], start=k == 0, stop=k == DK - 1)
                    op.then_inc(s["k2v2_done"], 1)
                    got(pe, "t2_split", b)
                    if isinstance(b, int) and b == 0:
                        pe.wait_ge(s["bias_ready"], 1)
                    got_if(pe, "q2_ready", b - 1)
                    op = project_q(q2ps, 3 * D, xnT[1])
                    op.then_inc(s["q2_done"], 1)
                if live(i - 4):
                    got(pe, "t3_copied", i - 4)
                    got_if(pe, "v_copied", i)
                    for t in range(TB):
                        for k in range(DK):
                            op = pe.matmul(lg_ps[:, t, :], xnT[2][:, k, tile(t)], wr[:, k, :], start=k == 0, stop=k == DK - 1)
                    op.then_inc(s["logits_done"], 1)

            pe.wait_ge(s["ident_set"], 1)
            steps(pe, step, LAG + 1, B)

            xrow16 = xrow.bitcast(F16)

            def routed_source(t, part, k):
                at = part * D + k * P
                return xrow16[:, t, at:at + P]

            def up(G, parity, e, f):
                c = FC * G + f
                if not (isinstance(c, int) and c < 2):
                    pe.wait_ge(s["gelu_done"], c - 1)
                x = xT[parity]
                for k in range(DK):
                    w_hi, w_lo = (w1[:, ds(e * 4096 + (k * 2048 + part * 1024 + f * P), P)] for part in range(2))
                    pe.matmul(hid[f % 2][:, 0:BLK], w_hi, x[:, k, 0, :], start=k == 0, stop=False)
                    pe.matmul(hid[f % 2][:, 0:BLK], w_hi, x[:, k, 1, :], start=False, stop=False)
                    op = pe.matmul(hid[f % 2][:, 0:BLK], w_lo, x[:, k, 0, :], start=False, stop=k == DK - 1)
                op.then_inc(s["up_done"], 1)

            def down(G, parity, e, f):
                c = FC * G + f
                got(pe, "g_ready", c)
                if f == 0 and not (isinstance(G, int) and G < 2):
                    pe.wait_ge(s["y_read"], G - 1)
                g = gs[f % 4]
                w_hi, w_lo = (w2[:, ds(e * 4096 + ((f // 4) * 2048 + part * 1024 + (f % 4) * 256), D)] for part in range(2))
                for t in range(TB):
                    y = ypair[parity][:, t, 0:D]
                    pe.matmul(y, g[:, 0, tile(t)], w_hi, start=f == 0, stop=False)
                    pe.matmul(y, g[:, 0, tile(t)], w_lo, start=False, stop=False)
                    op = pe.matmul(y, g[:, 1, tile(t)], w_hi, start=False, stop=f == FC - 1)
                op.then_inc(s["down_done"], 1)

            held = [E]

            def body(G, parity, routed, before, at_start=False):
                def expert_of(n):
                    return pe.value_load(blk_expert[0:1, ds(n, 1)], min_val=0, max_val=E - 1)

                if isinstance(G, int) and G == NSH:
                    pe.wait_ge(s["routed"], 1)
                    pe.wait_ge(s["last_lo"], 8)
                e = expert_of(G - NSH) if routed else E
                if before != "routed":
                    e_before = E
                else:
                    e_before = expert_of(G - (NSH + 1)) if at_start else held[0]
                held[0] = e
                for f in range(FC):
                    if f == 0:
                        got(pe, "xT_ready", G)
                    up(G, parity, e, f)
                    if f >= 2:
                        down(G, parity, e, f - 2)
                    elif before is not None:
                        down(G - 1, 1 - parity, e_before, FC - 2 + f)
                    if f == 1 and isinstance(G, int) and G == 0:
                        pe.wait_ge(s["x2_ready"], B)
                        pe.wait_ge(s["logits_copied"], B)
                        pe.wait_ge(s["xf_ready"], B)
                        pe.wait_ge(s["ident_set"], 2)
                        pe.wait_ge(s["ones_set"], 1)
                        pe.wait_ge(s["picked_ready"], 1)
                        pe.matmul(count_ps[:, 0, :], earlier[:, :], picked, start=True, stop=True)
                        pe.matmul(count_ps[:, 1, :], ones16[:, :], picked, start=True, stop=True)\
                            .then_inc(s["counts_done"], 1)
                    if f == 4 and not is_last(G):
                        if next_kind(G, routed) == "routed":
                            pe.wait_ge(s["xrow_loaded"], 16 * (G + (2 - NSH)))
                            transpose_rows(routed_source)
                        else:
                            transpose_rows(shared_source(G + 1))
                if is_last(G):
                    for f in range(FC - 2, FC):
                        down(G, parity, e, f)

            pe.wait_ge(s["w1_lo"], HALVES - 4)
            pe.wait_ge(s["w2_lo"], HALVES - 4)
            stream(pe, body)


_INS = ['x', 'ctx_1024', 'L0_attn_W', 'L0_xattn_Wq', 'L0_xattn_bq', 'L0_xattn_Wk', 'L0_xattn_bk', 'L0_xattn_Wv',
        'L0_xattn_bv', 'L0_ffn_Wfc_s', 'L0_ffn_bfc_s', 'L0_ffn_Wproj_s', 'L0_ffn_bproj_s', 'L0_ffn_Wr',
        'L0_ffn_Wfc', 'L0_ffn_bfc', 'L0_ffn_Wproj', 'L0_ffn_bproj']


def kernel(**inputs):
    import numpy as np
    import concourse.bacc as bacc
    from concourse.bass_utils import run_bass_kernel_spmd

    nc = bacc.Bacc("TRN2", target_bir_lowering=False, num_devices=1)
    arrays, args = {}, []
    for name in _INS:
        a = np.ascontiguousarray(inputs[name])
        arrays["in_" + name] = a
        args.append(nc.dram_tensor("in_" + name, a.shape, mybir.dt.from_np(a.dtype), kind="ExternalInput").ap())
    out = nc.dram_tensor("out", inputs["x"].shape, F32, kind="ExternalOutput").ap()
    decoder_layer(nc, *args, out)
    r = run_bass_kernel_spmd(nc, [arrays], core_ids=[0])
    return r.results[0]["out"]
```
